# Optimizing a Trainium2 kernel written in Bass

```python
import numpy as np
import jax
import jax.numpy as jnp

def _softmax(x, axis=-1):
    return jax.nn.softmax(x, axis=axis)

def _gelu(x):
    return jax.nn.gelu(x, approximate=True)

def _silu(x):
    return jax.nn.silu(x)

def _sigmoid(x):
    return jax.nn.sigmoid(x)

def _layernorm(x, axis=-1, eps=1e-05):
    m = jnp.mean(x, axis=axis, keepdims=True)
    v = jnp.var(x, axis=axis, keepdims=True)
    return (x - m) / jnp.sqrt(v + eps)

def _scatter_add(tgt, idx, src, axis=0):
    return tgt.at[idx].add(src)

def _segment_sum(src, seg, n):
    return jax.ops.segment_sum(src, seg, n)
kernel_name = 'mk_flamingo_gated_d1_seqx_r2_ec52dd'

def setup_inputs(seed: int=0):
    np.random.seed(seed)
    _w = jnp.asarray

    def _rec_inputs():
        import jax
        import jax.numpy as jnp
        _rk = jax.random.key(seed)
        x = -0.0002928 + 1 * jax.random.normal(jax.random.fold_in(_rk, 1), (16, 512, 512), jnp.float32)
        _lenS = 512 - jax.random.randint(jax.random.fold_in(_rk, 7), (16,), 0, max(1, 512 // 4) + 1, jnp.int32)
        _lenS2 = 120 - jax.random.randint(jax.random.fold_in(_rk, 8), (16,), 0, max(1, 120 // 4) + 1, jnp.int32)
        _ctx_1024P = jax.random.normal(jax.random.fold_in(_rk, 11), (16, 16, 512), jnp.float32)
        _ctx_1024c = jax.random.dirichlet(jax.random.fold_in(_rk, 511), 0.3 * jnp.ones((16,), jnp.float32), (16, 120))
        _ctx_1024t = jnp.einsum('bsk,bkd->bsd', _ctx_1024c, _ctx_1024P)
        _ctx_1024t = _ctx_1024t * jax.lax.rsqrt(jnp.mean(jnp.square(_ctx_1024t)) + 1e-12) * 0.953939
        ctx_1024 = 4.13588e-05 + 0.999923 * (_ctx_1024t + 0.3 * jax.random.normal(jax.random.fold_in(_rk, 611), (16, 120, 512), jnp.float32))
        itok_BxS_8_8191 = jax.random.randint(jax.random.fold_in(_rk, 12), (16, 512), 8, 4096, jnp.int32)
        itok_BxS2_1_8191 = jax.random.randint(jax.random.fold_in(_rk, 13), (16, 120), 1, 4096, jnp.int32)
        _validS = jnp.arange(512)[None, :] < _lenS[:, None]
        _validS2 = jnp.arange(120)[None, :] < _lenS2[:, None]
        _causal = jnp.tril(jnp.ones((512, 512), dtype=bool))
        mask_BxSxS2_if1 = jnp.where(jnp.ones((16, 512, 120), dtype=bool), 1, 0).astype(jnp.int32)
        _g = jax.random.normal(jax.random.fold_in(_rk, 9001), (2, 1), jnp.float32)
        _g = jnp.sign(_g) * jnp.maximum(jnp.abs(_g), 1.0) + (_g == 0) * 1.0
        g_xattn = _g[0]
        g_ffn = _g[1]
        return (x, ctx_1024, itok_BxS_8_8191, itok_BxS2_1_8191, mask_BxSxS2_if1, g_xattn, g_ffn)
    x, ctx_1024, itok_BxS_8_8191, itok_BxS2_1_8191, mask_BxSxS2_if1, g_xattn, g_ffn = _rec_inputs()

    def _L0_xattn_setup():
        import jax, jax.numpy as jnp
        import numpy as np
        DIM = 512
        NUM_HEADS = 16
        HEAD_DIM = DIM // NUM_HEADS

        def _slopes(num_heads):
            ratio = 2.0 ** (-8.0 / num_heads)
            return jnp.asarray([ratio ** i for i in range(1, num_heads + 1)], dtype=jnp.float32)
        key = jax.random.key(seed)
        ks = jax.random.split(key, 10)
        b, q_len, k_len = (2, 1024, 2048)
        query = jax.random.normal(ks[0], (b, q_len, DIM), dtype=jnp.float32)
        keys = jax.random.normal(ks[1], (b, k_len, DIM), dtype=jnp.float32)
        values = jax.random.normal(ks[2], (b, k_len, DIM), dtype=jnp.float32)
        query_pos = jnp.sort(jax.random.randint(ks[3], (b, q_len), 0, 4096), axis=-1)
        key_pos = jnp.sort(jax.random.randint(ks[4], (b, k_len), 0, 4096), axis=-1)
        mask = jnp.ones((b, q_len, k_len), dtype=jnp.int32)
        lim = float(np.sqrt(6.0 / (DIM + DIM)))
        W_q = jax.random.uniform(ks[5], (DIM, DIM), minval=-lim, maxval=lim, dtype=jnp.float32)
        W_k = jax.random.uniform(ks[6], (DIM, DIM), minval=-lim, maxval=lim, dtype=jnp.float32)
        W_v = jax.random.uniform(ks[7], (DIM, DIM), minval=-lim, maxval=lim, dtype=jnp.float32)
        W_o = jax.random.uniform(ks[8], (DIM, DIM), minval=-lim, maxval=lim, dtype=jnp.float32)
        return {'query': query, 'keys': keys, 'values': values, 'W_q': W_q, 'W_k': W_k, 'W_v': W_v, 'W_o': W_o, 'query_pos': query_pos, 'key_pos': key_pos, 'mask': mask}
    _L0_xattn_all = _L0_xattn_setup()
    _L0_xattn_in = {k: v for k, v in _L0_xattn_all.items() if k in ('W_q', 'W_k', 'W_v', 'W_o')}
    del _L0_xattn_all

    def _L0_ffn_setup():
        import jax, jax.numpy as jnp
        import numpy as np
        DIM = 512

        def _reference_tuple_inner(x, W_r, W_k, W_v, mu_r, mu_k):
            B, T, C = x.shape
            x_prev = jnp.concatenate([jnp.zeros((B, 1, C), x.dtype), x[:, :-1, :]], axis=1)
            xr = mu_r * x + (1.0 - mu_r) * x_prev
            xk = mu_k * x + (1.0 - mu_k) * x_prev
            r = jax.nn.sigmoid(jnp.einsum('btc,dc->btd', xr, W_r))
            k = jnp.einsum('btc,dc->btd', xk, W_k)
            k_act = jnp.square(jax.nn.relu(k))
            out = r * jnp.einsum('btc,dc->btd', k_act, W_v)
            new_state = x[:, -1, :]
            return (out, new_state)
        key = jax.random.key(seed)
        ks = jax.random.split(key, 6)
        B, T, C = (8, 1024, DIM)
        x = jax.random.normal(ks[0], (B, T, C), dtype=jnp.float32)
        s = 1.0 / np.sqrt(C)
        W_r = jax.random.uniform(ks[1], (C, C), jnp.float32, -s, s)
        W_k = jax.random.uniform(ks[2], (C, C), jnp.float32, -s, s)
        W_v = jax.random.uniform(ks[3], (C, C), jnp.float32, -s, s)
        mu_r = jax.random.uniform(ks[4], (C,), jnp.float32)
        mu_k = jax.random.uniform(ks[5], (C,), jnp.float32)
        return {'x': x, 'W_r': W_r, 'W_k': W_k, 'W_v': W_v, 'mu_r': mu_r, 'mu_k': mu_k}
    _L0_ffn_all = _L0_ffn_setup()
    _L0_ffn_in = {k: v for k, v in _L0_ffn_all.items() if k in ('W_r', 'W_k', 'W_v', 'mu_r', 'mu_k')}
    del _L0_ffn_all
    return {'x': x, 'ctx_1024': ctx_1024, 'itok_BxS_8_8191': itok_BxS_8_8191, 'itok_BxS2_1_8191': itok_BxS2_1_8191, 'mask_BxSxS2_if1': mask_BxSxS2_if1, 'g_xattn': g_xattn, 'g_ffn': g_ffn, 'L0_xattn_W_q': _L0_xattn_in['W_q'], 'L0_xattn_W_k': _L0_xattn_in['W_k'], 'L0_xattn_W_v': _L0_xattn_in['W_v'], 'L0_xattn_W_o': _L0_xattn_in['W_o'], 'L0_ffn_W_r': _L0_ffn_in['W_r'], 'L0_ffn_W_k': _L0_ffn_in['W_k'], 'L0_ffn_W_v': _L0_ffn_in['W_v'], 'L0_ffn_mu_r': _L0_ffn_in['mu_r'], 'L0_ffn_mu_k': _L0_ffn_in['mu_k']}

def reference(x, ctx_1024, itok_BxS_8_8191, itok_BxS2_1_8191, mask_BxSxS2_if1, g_xattn, g_ffn, L0_xattn_W_q, L0_xattn_W_k, L0_xattn_W_v, L0_xattn_W_o, L0_ffn_W_r, L0_ffn_W_k, L0_ffn_W_v, L0_ffn_mu_r, L0_ffn_mu_k):
    import jax
    import jax.numpy as jnp

    def _L0_xattn_ref(query, keys, values, W_q, W_k, W_v, W_o, query_pos, key_pos, mask):
        import jax, jax.numpy as jnp
        import numpy as np
        DIM = 512
        NUM_HEADS = 16
        HEAD_DIM = DIM // NUM_HEADS

        def _slopes(num_heads):
            ratio = 2.0 ** (-8.0 / num_heads)
            return jnp.asarray([ratio ** i for i in range(1, num_heads + 1)], dtype=jnp.float32)
        b, q_len, _ = query.shape
        k_len = keys.shape[1]
        scale = 1.0 / np.sqrt(HEAD_DIM)
        Q = (query @ W_q.T).reshape(b, q_len, NUM_HEADS, HEAD_DIM).transpose(0, 2, 1, 3)
        K = (keys @ W_k.T).reshape(b, k_len, NUM_HEADS, HEAD_DIM).transpose(0, 2, 1, 3)
        V = (values @ W_v.T).reshape(b, k_len, NUM_HEADS, HEAD_DIM).transpose(0, 2, 1, 3)
        scores = jnp.einsum('bhqd,bhkd->bhqk', Q, K) * scale
        dist = (query_pos[:, :, None] - key_pos[:, None, :]).astype(scores.dtype)
        bias = -_slopes(NUM_HEADS)[None, :, None, None] * dist[:, None, :, :]
        scores = scores + bias
        scores = jnp.where(mask[:, None, :, :] == 0, -jnp.inf, scores)
        m = jnp.max(scores, axis=-1, keepdims=True)
        e = jnp.exp(scores - m)
        attn = e / (1.0 + jnp.sum(e, axis=-1, keepdims=True))
        out = jnp.einsum('bhqk,bhkd->bhqd', attn, V)
        out = out.transpose(0, 2, 1, 3).reshape(b, q_len, DIM)
        return out @ W_o.T

    def _L0_ffn_ref(x, W_r, W_k, W_v, mu_r, mu_k):
        import jax, jax.numpy as jnp
        import numpy as np
        DIM = 512

        def _reference_tuple_inner(x, W_r, W_k, W_v, mu_r, mu_k):
            B, T, C = x.shape
            x_prev = jnp.concatenate([jnp.zeros((B, 1, C), x.dtype), x[:, :-1, :]], axis=1)
            xr = mu_r * x + (1.0 - mu_r) * x_prev
            xk = mu_k * x + (1.0 - mu_k) * x_prev
            r = jax.nn.sigmoid(jnp.einsum('btc,dc->btd', xr, W_r))
            k = jnp.einsum('btc,dc->btd', xk, W_k)
            k_act = jnp.square(jax.nn.relu(k))
            out = r * jnp.einsum('btc,dc->btd', k_act, W_v)
            new_state = x[:, -1, :]
            return (out, new_state)
        return _reference_tuple_inner(x, W_r, W_k, W_v, mu_r, mu_k)[0]
    x = x + jnp.tanh(g_xattn[0]) * _L0_xattn_ref(_layernorm(x, axis=-1), ctx_1024, ctx_1024, L0_xattn_W_q, L0_xattn_W_k, L0_xattn_W_v, L0_xattn_W_o, itok_BxS_8_8191, itok_BxS2_1_8191, mask_BxSxS2_if1)
    x = x + jnp.tanh(g_ffn[0]) * _L0_ffn_ref(_layernorm(x, axis=-1), L0_ffn_W_r, L0_ffn_W_k, L0_ffn_W_v, L0_ffn_mu_r, L0_ffn_mu_k)
    return x

_drawn_inputs = setup_inputs


def setup_inputs(seed=0):
    import zlib

    import numpy as np

    out = dict(_drawn_inputs(seed))
    spreads = {}
    factors = {'L0_ffn_W_r': 3.33, 'L0_ffn_mu_r': 7.415}
    for name, (base, spread) in spreads.items():
        noise = np.random.default_rng([zlib.crc32(name.encode()), seed]).standard_normal(out[name].shape)
        drawn = base * np.exp(spread * noise) if base else spread * noise
        out[name] = jnp.asarray(drawn.astype(out[name].dtype))
    for name, factor in factors.items():
        out[name] = (out[name] * factor).astype(out[name].dtype)
    return out
```

```python
from contextlib import ExitStack

import numpy as np

import concourse.bass as bass
from concourse import mybir

F32 = mybir.dt.float32
F32R = mybir.dt.float32r
I32 = mybir.dt.int32
ALU = mybir.AluOpType
ACT = mybir.ActivationFunctionType
AX = mybir.AxisListType

P = 128
HI, LO = 0, 1

SPLIT_PASSES = ((HI, HI), (HI, LO), (LO, HI))

ATTENTION_AND_FFN = (
    ("key", 0, -1), ("key", 1, -1), ("key", 2, -1), ("key", 3, -1),
    ("gate", 0, -1), ("value", 0, -1), ("gate", 1, -1), ("proj", 0, 0), ("value", 1, -1),
    ("gate", 2, -1), ("proj", 1, 0), ("value", 2, -1), ("turn2", 0, 0),
    ("gate", 3, -1), ("proj", 2, 0), ("value", 3, -1), ("turn1", 0, 1), ("turn1", 1, 1),
    ("turn1", 2, 1), ("turn2", 1, 0), ("turn1", 3, 1), ("proj", 3, 0), ("query", 0, 1),
    ("turn2", 2, 0), ("query", 1, 1), ("query", 2, 1), ("turn2", 3, 0), ("query", 3, 1),
)


def flamingo_block(nc, x, ctx_t, qpos, kpos, mask, g_xattn, g_ffn, wq, wk, wv, wo,
                   ffn_wr, ffn_wk, ffn_wv, mu_r, mu_k, out):
    NB, S, D = x.shape
    NK = kpos.shape[1]
    H = 16
    HD = D // H
    QT = S // P
    CT = D // P
    G = CT
    J = P // HD
    CB = 2
    CK = CB * NK
    EPS = 1e-5
    BIG = 1e30
    SCALE = 1.0 / float(np.sqrt(HD))
    RATIO = 2.0 ** (-8.0 / H)
    SLOPES = [float(np.float32(RATIO ** i)) for i in range(1, H + 1)]
    assert S == 512 and D == 512 and NB % (2 * CB) == 0 and NB > 2

    key_scratch = nc.dram_tensor("key_scratch", (NB, P, CT, NK), F32, kind="Internal").ap()
    value_scratch = nc.dram_tensor("value_scratch", (NB, NK, D), F32, kind="Internal").ap()

    with ExitStack() as stack:
        def sb(name, shape, dt=F32):
            return stack.enter_context(nc.sbuf_tensor(name, shape, dt))

        def sem(name):
            return stack.enter_context(nc.semaphore(name))

        w_query, w_proj, w_gate, w_key, w_value = (
            sb(n, [P, 2, CT, D], F32R) for n in ("w_query", "w_proj", "w_gate", "w_key", "w_value"))
        xs = sb("xs", [P, 2, QT, D])
        norm1 = sb("norm1", [P, D])
        norm2 = sb("norm2", [P, 2, D])
        xnt_or_act = sb("xnt_or_act", [P, 2, CT, S], F32R)
        mixed_key = sb("mixed_key", [P, 2, CT, S], F32R)
        mixed_gate = sb("mixed_gate", [P, 2, CT, S], F32R)
        xn2t = sb("xn2t", [P, 2, CT, 1 + P])
        diff = sb("diff", [P, CT, P])
        mix_g = sb("mix_g", [P, CT, P])
        query_t = sb("query_t", [P, CT, S])
        probs = sb("probs", [P, 2, H, NK])
        probs_t = sb("probs_t", [NK, 2, J, P])
        attn_t = sb("attn_t", [P, 2, G, P], F32R)
        keys_t = sb("keys_t", [P, CT, NK])
        values = sb("values", [NK, D])
        gated = sb("gated", [P, 2, D])
        relu = sb("relu", [P, S])
        square = sb("square", [P, S])
        mask_in = sb("mask_in", [P, QT, NK], I32)
        kpos_in = sb("kpos_in", [P, NK], I32)
        kpos_f = sb("kpos_f", [P, NK])
        neg_dist = sb("neg_dist", [P, QT, NK])
        qpos_in = sb("qpos_in", [P, NB, QT], I32)
        qpos_f = sb("qpos_f", [P, NB, QT])
        ident = sb("ident", [P, P])
        mu = sb("mu", [P, 2, CT])
        gates_in = sb("gates_in", [P, 2])
        gates = sb("gates", [P, 2])
        half_gate = sb("half_gate", [P, 1])
        stats1 = sb("stats1", [P, QT, 6])
        stats2 = sb("stats2", [P, 6])
        mv1 = sb("mv1", [P, QT, 2])
        rstd1 = sb("rstd1", [P, QT])
        mv2 = sb("mv2", [P, 2])
        rstd2 = sb("rstd2", [P, 1])
        power = sb("power", [P, QT])
        neg_max = sb("neg_max", [P, 2, H])
        sums = sb("sums", [P, 2, H])
        sums1 = sb("sums1", [P, 2, H])
        recip = sb("recip", [P, 2, H])

        wk_split = mixed_key
        wv_split = mixed_gate
        ctx_raw = probs[:].rearrange("p a h k -> p (a h k)").rearrange("p (a c k) -> p a c k", a=4, k=CK)
        ctx_split = [xnt_or_act[:].rearrange("p s c t -> p (s c t)")[:, i * 2 * CT * CK:(i + 1) * 2 * CT * CK]
                     .rearrange("p (s c k) -> p s c k", s=2, c=CT) for i in range(2)]
        key_out = query_t[:].rearrange("p c t -> p (c t)").rearrange("p (a c k) -> p a c k", a=2, c=CT)[:, :, :, 0:CK]
        value_out = gated

        score_banks = [stack.enter_context(nc.psum_tensor(f"score_bank{j}", [P, 512], F32)) for j in range(J)]
        rotating = [stack.enter_context(nc.psum_tensor(f"rotating{i}", [P, 512], F32)) for i in range(2)]
        probs_bank = stack.enter_context(nc.psum_tensor("probs_bank", [P, 512], F32))
        attn_bank = stack.enter_context(nc.psum_tensor("attn_bank", [P, 512], F32))
        bank_of = {(what, tile): rotating[i % 2] for i, (what, tile, _) in enumerate(ATTENTION_AND_FFN)}
        without_ffn = [u for u in ATTENTION_AND_FFN if u[2] >= 0]

        small_loaded = sem("small_loaded")
        raw_weight = [sem(f"raw_weight{i}") for i in range(2)]
        ctx_loaded = [sem(f"ctx_loaded{i}") for i in range(2)]
        x_loaded = [sem(f"x_loaded{t}") for t in range(QT)]
        mask_loaded = sem("mask_loaded")
        keys_loaded = sem("keys_loaded")
        values_loaded = sem("values_loaded")
        keys_stored = [sem(f"keys_stored{i}") for i in range(2)]
        gated_stored = [sem(f"gated_stored{i}") for i in range(2)]
        ident_zero = sem("ident_zero")
        consts_ready = sem("consts_ready")
        gates_ready = sem("gates_ready")
        weight_high = sem("weight_high")
        weight_low = sem("weight_low")
        ctx_high = sem("ctx_high")
        ctx_low = sem("ctx_low")
        kproj_done = sem("kproj_done")
        kproj_read = sem("kproj_read")
        vproj_done = sem("vproj_done")
        vproj_read = sem("vproj_read")
        done = {k: sem(f"{k}_done") for k in ("key", "gate", "value", "proj", "query", "turn1", "turn2")}
        read = {k: sem(f"{k}_read") for k in ("key", "gate", "value", "proj", "query", "turn1", "turn2")}
        turn1_high = sem("turn1_high")
        scores_done = sem("scores_done")
        scores_biased = sem("scores_biased")
        max_ready = sem("max_ready")
        exp_done = sem("exp_done")
        sum_ready = sem("sum_ready")
        recip_ready = sem("recip_ready")
        probs_ready = sem("probs_ready")
        probs_turned = sem("probs_turned")
        probs_t_ready = sem("probs_t_ready")
        attn_done = sem("attn_done")
        attn_high = sem("attn_high")
        attn_read = sem("attn_read")
        dist_mask = sem("dist_mask")
        dist_plain = sem("dist_plain")
        dist_ready = sem("dist_ready")
        stats1_part = sem("stats1_part")
        stats1_ready = sem("stats1_ready")
        var1_ready = sem("var1_ready")
        rstd1_ready = sem("rstd1_ready")
        norm1_ready = sem("norm1_ready")
        x2_ready = sem("x2_ready")
        stats2_part = sem("stats2_part")
        stats2_ready = sem("stats2_ready")
        var2_ready = sem("var2_ready")
        rstd2_ready = sem("rstd2_ready")
        norm2_ready = sem("norm2_ready")
        edge_ready = sem("edge_ready")
        diff_ready = sem("diff_ready")
        mixg_ready = sem("mixg_ready")
        mixk_ready = sem("mixk_ready")
        mixg_high = sem("mixg_high")
        mixk_high = sem("mixk_high")
        mixg_low = sem("mixg_low")
        mixk_low = sem("mixk_low")
        square_ready = sem("square_ready")
        act_high = sem("act_high")
        act_low = sem("act_low")
        gated_part = sem("gated_part")
        out_ready = sem("out_ready")

        raw = [wk, wv, wq, ffn_wk, ffn_wr, ffn_wv, wo]
        split = [wk_split, wv_split, w_query, w_key, w_gate, w_value, w_proj]
        NCHUNK = NB // CB

        def sub(b, k):
            return b - k

        def apart(engine):
            engine.nop(nofuse=True)

        block = stack.enter_context(nc.Block())

        @block.sync
        def _(sp):
            for dst, src in ((qpos_in[:].rearrange("p b t -> p (b t)"), qpos), (mu[:, 0, :], mu_r), (mu[:, 1, :], mu_k),
                             (gates_in[:, 0:1], g_xattn.rearrange("(a n) -> a n", a=1).to_broadcast((P, 1))),
                             (gates_in[:, 1:2], g_ffn.rearrange("(a n) -> a n", a=1).to_broadcast((P, 1)))):
                sp.dma_start(dst, src).then_inc(small_loaded, 16)

            def load_weight(i):
                if i >= 2:
                    sp.wait_ge(weight_low, i - 1)
                sp.dma_start(xs[:, i % 2], raw[i].rearrange("(c p) n -> p c n", p=P)).then_inc(raw_weight[i % 2], 16)

            def load_ctx(chunk, i, wait=None):
                if wait is not None:
                    sp.wait_ge(ctx_low, wait)
                sp.dma_start(ctx_raw[:, i], ctx_t[:, bass.ds(chunk * CK, CK)].rearrange("(c p) k -> p c k", p=P))\
                    .then_inc(ctx_loaded[i], 16)

            def store_chunk(n, i):
                sp.wait_ge(kproj_read, n * 2 * CT + (i + 1) * CT)
                for b in range(CB):
                    sp.dma_start(key_scratch[bass.ds((n * 2 + i) * CB + b, 1)].rearrange("b p c k -> p (b c) k"),
                                 key_out[:, i, :, b * NK:(b + 1) * NK]).then_inc(keys_stored[i], 16)
                for b in range(CB):
                    sp.wait_ge(vproj_read, n * 2 * CB + i * CB + b + 1)
                    sp.dma_start(value_scratch[bass.ds((n * 2 + i) * CB + b, 1)].rearrange("b k d -> (b k) d"),
                                 value_out[0:NK, b, :]).then_inc(gated_stored[b], 16)

            load_ctx(0, 0)
            load_weight(0)
            load_weight(1)
            load_ctx(1, 1)
            for i in range(2, len(raw)):
                load_weight(i)
            with sp.Fori(0, NCHUNK // 2 - 1) as n:
                for i in range(2):
                    load_ctx(n * 2 + 2 + i, i, wait=n * 2 + i + 1)
                    store_chunk(n, i)
            for i in range(2):
                store_chunk(NCHUNK // 2 - 1, i)
            for i in range(2):
                sp.wait_ge(keys_stored[i], 16 * CB * (NCHUNK // 2))
                sp.wait_ge(gated_stored[i], 16 * NCHUNK)

            def load_x(b, t):
                sp.dma_start(xs[:, bass.ds(b % 2, 1), t].rearrange("p a d -> p (a d)"),
                             x[bass.ds(b, 1), t * P:(t + 1) * P, :].rearrange("b p d -> (b p) d")).then_inc(x_loaded[t], 16)

            def load_mask(b):
                sp.dma_start(mask_in[:], mask[bass.ds(b, 1)].rearrange("b (t p) k -> p (b t) k", p=P))\
                    .then_inc(mask_loaded, 16)
                sp.dma_start(kpos_in[:], kpos[bass.ds(b, 1)].to_broadcast((P, NK))).then_inc(mask_loaded, 16)

            def load_keys(b):
                sp.dma_start(keys_t[:], key_scratch[bass.ds(b, 1)].rearrange("b p c k -> p (b c) k")).then_inc(keys_loaded, 16)

            def load_values(b):
                sp.dma_start(values[:], value_scratch[bass.ds(b, 1)].rearrange("b k d -> (b k) d"))\
                    .then_inc(values_loaded, 16)

            def store_out(b, t):
                sp.wait_ge(out_ready, b * QT + t + 1)
                sp.dma_start(out[bass.ds(b, 1), t * P:(t + 1) * P, :].rearrange("b p d -> (b p) d"),
                             gated[:, t % 2]).then_inc(gated_stored[t % 2], 16)

            sp.wait_ge(weight_low, len(raw))
            for t in range(QT):
                load_x(0, t)
            load_mask(0)
            load_keys(0)
            load_values(0)

            def batch(b, ffn, last):
                if not ffn:
                    sp.wait_ge(stats1_ready, QT)
                    for t in range(QT):
                        load_x(b + 1, t)
                if not last:
                    sp.wait_ge(dist_ready, b + 1)
                    load_mask(b + 1)
                for t in range(QT):
                    if ffn:
                        store_out(b - 1, t)
                        if not last:
                            load_x(b + 1, t)
                if not last:
                    sp.wait_ge(scores_done, (b + 1) * QT)
                    load_keys(b + 1)
                    sp.wait_ge(attn_done, (b + 1) * QT)
                    load_values(b + 1)

            batch(0, False, False)
            with sp.Fori(1, NB - 1) as b:
                batch(b, True, False)
            batch(NB - 1, True, True)
            for t in range(QT):
                store_out(NB - 1, t)
            for i in range(2):
                sp.wait_ge(gated_stored[i], 16 * (NCHUNK + NB * QT // 2))

        @block.tensor
        def _(pe):
            def product(bank, stationary, moving, steps=range(CT)):
                mm = None
                for c in steps:
                    for n, (a, b) in enumerate(SPLIT_PASSES):
                        mm = pe.matmul(bank, stationary(a, c), moving(b, c), start=(c == 0 and n == 0),
                                       stop=(c == CT - 1 and n == len(SPLIT_PASSES) - 1))
                return mm

            pe.wait_ge(consts_ready, 1)

            def chunk(n, i, first):
                pe.wait_ge(ctx_low, n * 2 + i + 1)
                for m in range(CT):
                    if m < 2 and not first:
                        pe.wait_ge(vproj_read, n * 2 * CB + i * CB - CB + m + 1)
                    if m >= 2:
                        pe.wait_ge(kproj_read, n * 2 * CT + i * CT + m - 1)
                    product(rotating[m % 2][:, 0:CK], lambda s, c: wk_split[:, s, c, m * P:(m + 1) * P],
                            lambda s, c: ctx_split[i][:, s, c, :]).then_inc(kproj_done, 1)
                if first:
                    pe.wait_ge(weight_low, 2)
                for b in range(CB):
                    pe.wait_ge(kproj_read, n * 2 * CT + i * CT + 3 + b)
                    product(rotating[b][0:NK, :], lambda s, c: ctx_split[i][:, s, c, b * NK:(b + 1) * NK],
                            lambda s, c: wv_split[:, s, c, :]).then_inc(vproj_done, 1)

            pe.wait_ge(weight_low, 1)
            chunk(0, 0, True)
            chunk(0, 1, False)
            with pe.Fori(1, NCHUNK // 2) as n:
                chunk(n, 0, False)
                chunk(n, 1, False)

            def free_bank(b, use, order, before):
                same = [u for u in before + order if bank_of[u[0], u[1]] is bank_of[use[0], use[1]]]
                own = len([u for u in before if u in same])
                at = own + [u for u in order if u in same].index(use)
                if at == 0:
                    return
                what, tile, rel = same[at - 1]
                if at - 1 < own:
                    rel -= 1
                pe.wait_ge(read[what], (b + rel) * 4 + tile + 1)

            def scores(b, t):
                if t == 0:
                    pe.wait_ge(read["query"], b * CT + CT)
                    pe.wait_ge(keys_loaded, b * 16 + 16)
                if isinstance(b, int) and b == 0 and t == 0:
                    pass
                else:
                    pe.wait_ge(scores_biased, (b * QT + t) * G)
                for g in range(G):
                    for j in range(J):
                        rows = slice(j * HD, (j + 1) * HD)
                        mm = pe.matmul(score_banks[j][:, g * NK:(g + 1) * NK], query_t[rows, g, t * P:(t + 1) * P],
                                       keys_t[rows, g, :], start=True, stop=True)
                mm.then_inc(scores_done, 1)

            def turn1(b, t):
                pe.wait_ge(norm1_ready, b * QT + t + 1)
                bank = bank_of["turn1", t]
                for c in range(CT):
                    mm = pe.transpose(bank[:, c * P:(c + 1) * P], norm1[:, c * P:(c + 1) * P], ident[:])
                mm.then_inc(done["turn1"], 1)

            def turn2(b, t):
                pe.wait_ge(norm2_ready, b * QT + t + 1)
                bank = bank_of["turn2", t]
                for c in range(CT):
                    mm = pe.transpose(bank[:, c * P:(c + 1) * P], norm2[:, t % 2, c * P:(c + 1) * P], ident[:])
                mm.then_inc(done["turn2"], 1)

            def query(b, m):
                if m == 0:
                    pe.wait_ge(read["turn1"], (b + 1) * QT)
                product(bank_of["query", m][:], lambda s, c: w_query[:, s, c, m * P:(m + 1) * P],
                        lambda s, c: xnt_or_act[:, s, c, :]).then_inc(done["query"], 1)

            def key(b, m):
                if m == 0:
                    pe.wait_ge(mixk_low, (b + 1) * QT)
                product(bank_of["key", m][:], lambda s, c: w_key[:, s, c, m * P:(m + 1) * P],
                        lambda s, c: mixed_key[:, s, c, :]).then_inc(done["key"], 1)

            def gate(b, t):
                if t == 0:
                    pe.wait_ge(mixg_low, (b + 1) * QT)
                product(bank_of["gate", t][:], lambda s, c: mixed_gate[:, s, c, t * P:(t + 1) * P],
                        lambda s, c: w_gate[:, s, c, :]).then_inc(done["gate"], 1)

            def value(b, t, steps):
                if t == 0 and steps[0] == 0:
                    pe.wait_ge(act_low, (b + 1) * CT)
                mm = product(bank_of["value", t][:], lambda s, c: xnt_or_act[:, s, c, t * P:(t + 1) * P],
                             lambda s, c: w_value[:, s, c, :], steps)
                if steps[-1] == CT - 1:
                    mm.then_inc(done["value"], 1)

            def proj(b, t):
                pe.wait_ge(attn_read, b * QT + t + 1)
                product(bank_of["proj", t][:], lambda s, c: attn_t[:, s, c, :],
                        lambda s, c: w_proj[:, s, c, :]).then_inc(done["proj"], 1)

            def turn_probs(b, t, g):
                pe.wait_ge(probs_ready, (b * QT + t) * 2 + g // 2 + 1)
                if not (isinstance(b, int) and b == 0 and t == 0 and g == 0):
                    pe.wait_ge(probs_t_ready, (b * QT + t) * G + g)
                for j in range(J):
                    mm = pe.transpose(probs_bank[0:NK, j * P:(j + 1) * P], probs[:, t % 2, g * J + j, :], ident[:])
                mm.then_inc(probs_turned, 1)

            def attend(b, t, g):
                pe.wait_ge(probs_t_ready, (b * QT + t) * G + g + 1)
                if g == 0:
                    if t == 0:
                        pe.wait_ge(values_loaded, b * 16 + 16)
                    if not (isinstance(b, int) and b == 0 and t == 0):
                        pe.wait_ge(attn_read, b * QT + t)
                for j in range(J):
                    head = g * J + j
                    mm = pe.matmul(attn_bank[j * HD:(j + 1) * HD, g * P:(g + 1) * P],
                                   values[:, head * HD:(head + 1) * HD], probs_t[:, g % 2, j, :],
                                   start=True, stop=True, skip_group_check=True)
                if g == G - 1:
                    mm.then_inc(attn_done, 1)

            def attention(b, t, ffn, order, before):
                if ffn:
                    free_bank(b, ("value", t, -1), order, before)
                for g in range(G):
                    turn_probs(b, t, g)
                    if ffn:
                        value(b - 1, t, [g])
                    if g > 0:
                        attend(b, t, g - 1)
                attend(b, t, G - 1)

            def batch(b, ffn, last, before):
                order = [u for u in ATTENTION_AND_FFN if (ffn or u[2] >= 0) and (not last or u[2] <= 0)]
                made = {"key": key, "gate": gate, "proj": proj, "turn1": turn1, "turn2": turn2, "query": query}

                def use(what, tile):
                    found = [u for u in order if u[:2] == (what, tile)]
                    if found:
                        free_bank(b, found[0], order, before)
                        made[what](b + found[0][2], tile)

                scores(b, 0)
                use("key", 0)
                use("key", 1)
                scores(b, 1)
                use("key", 2)
                use("key", 3)
                use("gate", 0)
                attention(b, 0, ffn, order, before)
                scores(b, 2)
                use("gate", 1)
                use("proj", 0)
                attention(b, 1, ffn, order, before)
                scores(b, 3)
                use("gate", 2)
                use("proj", 1)
                attention(b, 2, ffn, order, before)
                use("turn2", 0)
                use("gate", 3)
                use("proj", 2)
                attention(b, 3, ffn, order, before)
                use("turn1", 0)
                use("turn1", 1)
                use("turn1", 2)
                use("turn2", 1)
                use("turn1", 3)
                use("proj", 3)
                use("query", 0)
                use("turn2", 2)
                use("query", 1)
                use("query", 2)
                use("turn2", 3)
                use("query", 3)
                return order

            pe.wait_ge(vproj_read, NB)
            pe.wait_ge(kproj_read, NCHUNK * CT)
            first = [u for u in ATTENTION_AND_FFN if u[0] in ("turn1", "query")]
            for u in first:
                free_bank(-1, u, first, [])
                {"turn1": turn1, "query": query}[u[0]](0, u[1])
            batch(0, False, False, first)
            full = list(ATTENTION_AND_FFN)
            with pe.Fori(1, NB - 1) as b:
                batch(b, True, False, full)
            batch(NB - 1, True, True, full)
            last_uses = [u for u in ATTENTION_AND_FFN if u[2] < 0]
            before = [u for u in ATTENTION_AND_FFN if u[2] <= 0]
            for u in last_uses:
                free_bank(NB, u, last_uses, before)
                if u[0] == "value":
                    value(NB - 1, u[1], range(CT))
                else:
                    {"key": key, "gate": gate}[u[0]](NB - 1, u[1])

        @block.scalar
        def _(act):
            act.wait_ge(small_loaded, 16 * 5)
            act.activation(gates[:], gates_in[:], ACT.Tanh).then_inc(gates_ready, 1)
            act.wait_ge(gates_ready, 1)
            act.mul(half_gate[:], gates[:, 1:2], 0.5).then_inc(gates_ready, 1)

            def weight(i):
                act.wait_ge(raw_weight[i % 2], 16 * (i // 2 + 1))
                act.copy(split[i][:, HI], xs[:, i % 2]).then_inc(weight_high, 1)

            def chunk(n, i, first, extra=None):
                act.wait_ge(ctx_loaded[i], 16 * n + 16)
                if not first:
                    act.wait_ge(vproj_done, n * 2 * CB + i * CB - CB)
                act.copy(ctx_split[i][:, HI], ctx_raw[:, i]).then_inc(ctx_high, 1)

            def keys_out(n, i, first):
                if not first:
                    act.wait_ge(keys_stored[i], 16 * CB * n)
                for m in range(CT):
                    act.wait_ge(kproj_done, n * 2 * CT + i * CT + m + 1)
                    act.copy(key_out[:, i, m, :], rotating[m % 2][:, 0:CK]).then_inc(kproj_read, 1)

            weight(0)
            chunk(0, 0, True)
            weight(1)
            chunk(0, 1, True)
            weight(2)
            keys_out(0, 0, True)
            weight(3)
            weight(4)
            keys_out(0, 1, True)
            weight(5)
            weight(6)
            with act.Fori(1, NCHUNK // 2) as n:
                for i in range(2):
                    chunk(n, i, False)
                    keys_out(n, i, False)

            def turn1_out(b, t):
                if t == 0 and not (isinstance(b, int) and b < 2):
                    act.wait_ge(done["value"], (b - 1) * QT)
                act.wait_ge(done["turn1"], b * QT + t + 1)
                act.copy(xnt_or_act[:, HI, :, t * P:(t + 1) * P],
                         bank_of["turn1", t][:].rearrange("p (c q) -> p c q", c=CT)).then_inc(turn1_high, 1)

            def query_out(b, m):
                act.wait_ge(done["query"], b * CT + m + 1)
                act.mul(query_t[:, m, :], bank_of["query", m][:], SCALE).then_inc(read["query"], 1)

            def exps(b, t, g):
                act.wait_ge(max_ready, (b * QT + t) * G + g + 1)
                for j in range(J):
                    head = g * J + j
                    e = act.activation(probs[:, t % 2, head, :], probs[:, t % 2, head, :], ACT.Exp,
                                       bias=neg_max[:, t % 2, head:head + 1],
                                       accum_out=sums[:, t % 2, head:head + 1])
                e.then_inc(exp_done, 1)

            def probs_out(b, t, g):
                act.wait_ge(probs_turned, (b * QT + t) * G + g + 1)
                act.copy(probs_t[:, g % 2], probs_bank[0:NK, :].rearrange("k (j q) -> k j q", j=J))\
                    .then_inc(probs_t_ready, 1)

            def attn_out(b, t):
                act.wait_ge(attn_done, b * QT + t + 1)
                if not (isinstance(b, int) and b == 0 and t == 0):
                    act.wait_ge(done["proj"], b * QT + t)
                act.copy(attn_t[:, HI], attn_bank[:].rearrange("p (g q) -> p g q", g=G)).then_inc(attn_high, 1)

            def turn2_out(b, t):
                act.wait_ge(done["turn2"], b * QT + t + 1)
                if not (isinstance(b, int) and b == 0 and t < 2):
                    act.wait_ge(mixk_ready, b * QT + t - 1)
                act.copy(xn2t[:, t % 2, :, 1:], bank_of["turn2", t][:].rearrange("p (c q) -> p c q", c=CT))\
                    .then_inc(read["turn2"], 1)

            def mix_high(b, t):
                act.wait_ge(mixg_ready, b * QT + t + 1)
                act.copy(mixed_gate[:, HI, :, t * P:(t + 1) * P], mix_g[:]).then_inc(mixg_high, 1)
                act.wait_ge(mixk_ready, b * QT + t + 1)
                act.copy(mixed_key[:, HI, :, t * P:(t + 1) * P], diff[:]).then_inc(mixk_high, 1)

            def relu_out(b, m):
                act.wait_ge(done["key"], b * CT + m + 1)
                act.activation(relu[:], bank_of["key", m][:], ACT.Relu).then_inc(read["key"], 1)

            def act_split(b, m):
                act.wait_ge(square_ready, b * CT + m + 1)
                act.copy(xnt_or_act[:, HI, m, :], square[:]).then_inc(act_high, 1)

            def gate_out(b, t):
                act.wait_ge(done["gate"], b * QT + t + 1)
                act.wait_ge(gated_stored[t % 2], (NCHUNK + b * 2 + t // 2) * 16)
                act.activation(gated[:, t % 2], bank_of["gate", t][:], ACT.Tanh, scale=0.5).then_inc(read["gate"], 1)

            def batch(b, ffn, last):
                f = sub(b, 1)
                if ffn:
                    for m in range(CT):
                        relu_out(f, m)
                        act_split(f, m)
                        exps(b, 0, m)
                    exps(b, 1, 0)
                    gate_out(f, 0)
                    exps(b, 1, 1)
                else:
                    for g in range(G):
                        exps(b, 0, g)
                    exps(b, 1, 0)
                    exps(b, 1, 1)
                for g in range(G):
                    probs_out(b, 0, g)
                attn_out(b, 0)
                exps(b, 1, 2)
                exps(b, 1, 3)
                if ffn:
                    gate_out(f, 1)
                exps(b, 2, 0)
                for g in range(G):
                    probs_out(b, 1, g)
                attn_out(b, 1)
                exps(b, 2, 1)
                exps(b, 2, 2)
                exps(b, 2, 3)
                if ffn:
                    gate_out(f, 2)
                exps(b, 3, 0)
                for g in range(G):
                    probs_out(b, 2, g)
                attn_out(b, 2)
                exps(b, 3, 1)
                turn2_out(b, 0)
                exps(b, 3, 2)
                exps(b, 3, 3)
                if ffn:
                    gate_out(f, 3)
                mix_high(b, 0)
                for g in range(G):
                    probs_out(b, 3, g)
                attn_out(b, 3)
                if not last:
                    turn1_out(b + 1, 0)
                    turn1_out(b + 1, 1)
                    turn1_out(b + 1, 2)
                turn2_out(b, 1)
                if not last:
                    turn1_out(b + 1, 3)
                mix_high(b, 1)
                if not last:
                    query_out(b + 1, 0)
                turn2_out(b, 2)
                mix_high(b, 2)
                if not last:
                    query_out(b + 1, 1)
                    query_out(b + 1, 2)
                turn2_out(b, 3)
                mix_high(b, 3)
                if not last:
                    query_out(b + 1, 3)

            for i in range(2):
                act.wait_ge(keys_stored[i], 16 * CB * (NCHUNK // 2))
                act.wait_ge(gated_stored[i], 16 * NCHUNK)
            act.wait_ge(vproj_done, NB)
            for t in range(QT):
                turn1_out(0, t)
            for m in range(CT):
                query_out(0, m)
            batch(0, False, False)
            with act.Fori(1, NB - 1) as b:
                batch(b, True, False)
            batch(NB - 1, True, True)
            for m in range(CT):
                relu_out(NB - 1, m)
                act_split(NB - 1, m)
            for t in range(QT):
                gate_out(NB - 1, t)

        @block.vector
        def _(dve):
            as_f32 = lambda ap: ap.bitcast(F32)
            dve.wait_ge(small_loaded, 16 * 5)
            dve.tensor_copy(qpos_f[:], qpos_in[:]).then_inc(consts_ready, 1)
            dve.memset(xn2t[:, 0, :, 0:1], 0.0).then_inc(edge_ready, 1)

            def weight(i):
                dve.wait_ge(weight_high, i + 1)
                dve.tensor_tensor(split[i][:, LO], xs[:, i % 2], as_f32(split[i][:, HI]), ALU.subtract)\
                    .then_inc(weight_low, 1)

            def chunk(n, i):
                dve.wait_ge(ctx_high, n * 2 + i + 1)
                dve.tensor_tensor(ctx_split[i][:, LO], ctx_raw[:, i], as_f32(ctx_split[i][:, HI]), ALU.subtract)\
                    .then_inc(ctx_low, 1)

            def values_out(n, i, first):
                for b in range(CB):
                    dve.wait_ge(vproj_done, n * 2 * CB + i * CB + b + 1)
                    if not first:
                        dve.wait_ge(gated_stored[b], (n * 2 + i) * 16)
                    dve.tensor_copy(value_out[0:NK, b, :], rotating[b][0:NK, :]).then_inc(vproj_read, 1)

            weight(0)
            chunk(0, 0)
            weight(1)
            chunk(0, 1)
            weight(2)
            values_out(0, 0, True)
            weight(3)
            weight(4)
            values_out(0, 1, False)
            weight(5)
            weight(6)
            with dve.Fori(1, NCHUNK // 2) as n:
                for i in range(2):
                    chunk(n, i)
                    values_out(n, i, False)

            def x_tile(b, t):
                return xs[:, bass.ds(b % 2, 1), t].rearrange("p a d -> p (a d)")

            def statistics1(b):
                if not (isinstance(b, int) and b == 0):
                    dve.wait_ge(stats1_ready, b * QT)
                for t in range(QT):
                    dve.wait_ge(x_loaded[t], b * 16 + 16)
                    apart(dve)
                    dve.bn_stats(stats1[:, t, :], x_tile(b, t)).then_inc(stats1_part, 1)
                if not (isinstance(b, int) and b == 0):
                    dve.wait_ge(var1_ready, b)
                    dve.wait_ge(norm1_ready, b * QT)
                for t in range(QT):
                    dve.wait_ge(stats1_part, b * QT + t + 1)
                    apart(dve)
                    dve.bn_aggr(mv1[:, t, :], stats1[:, t, :]).then_inc(stats1_ready, 1)

            def normalise1(b, t):
                if t == 0:
                    dve.wait_ge(rstd1_ready, b + 1)
                if not (isinstance(b, int) and b == 0 and t == 0):
                    dve.wait_ge(done["turn1"], b * QT + t)
                dve.tensor_scalar(norm1[:], x_tile(b, t), mv1[:, t, 0:1], rstd1[:, t:t + 1], ALU.subtract, ALU.mult)\
                    .then_inc(norm1_ready, 1)

            def turn1_low(b, t):
                dve.wait_ge(turn1_high, b * QT + t + 1)
                part = xnt_or_act[:, :, :, t * P:(t + 1) * P]
                dve.tensor_tensor(part[:, LO], bank_of["turn1", t][:].rearrange("p (c q) -> p c q", c=CT),
                                  as_f32(part[:, HI]), ALU.subtract).then_inc(read["turn1"], 1)

            def bias(b, t, g):
                if g == 0:
                    dve.wait_ge(scores_done, b * QT + t + 1)
                    if t == 0:
                        dve.wait_ge(dist_ready, b + 1)
                    if not (isinstance(b, int) and b == 0 and t < 2):
                        dve.wait_ge(probs_turned, (b * QT + t - 1) * G)
                        dve.wait_ge(exp_done, (b * QT + t - 1) * G)
                for j in range(J):
                    head = g * J + j
                    z = dve.scalar_tensor_tensor(out=probs[:, t % 2, head, :], in0=neg_dist[:, t, :], scalar=SLOPES[head],
                                                 in1=score_banks[j][:, g * NK:(g + 1) * NK], op0=ALU.mult, op1=ALU.add)
                z.then_inc(scores_biased, 1)
                dve.wait_ge(scores_biased, (b * QT + t) * G + g + 1)
                dve.tensor_reduce(neg_max[:, t % 2, g * J:(g + 1) * J], probs[:, t % 2, g * J:(g + 1) * J, :],
                                  AX.X, ALU.max, negate=True).then_inc(max_ready, 1)

            def reciprocals(b, t, half):
                heads = slice(half * H // 2, (half + 1) * H // 2)
                at = (b * QT + t) * 2 + half + 1
                dve.wait_ge(exp_done, (b * QT + t) * G + half * 2 + 2)
                if half == 0 and not (isinstance(b, int) and b == 0 and t < 2):
                    dve.wait_ge(probs_ready, (b * QT + t - 1) * 2)
                dve.tensor_scalar(sums1[:, t % 2, heads], sums[:, t % 2, heads], 1.0, None, ALU.add).then_inc(sum_ready, 1)
                dve.wait_ge(sum_ready, at)
                dve.reciprocal(recip[:, t % 2, heads], sums1[:, t % 2, heads]).then_inc(recip_ready, 1)

            def attn_low(b, t):
                dve.wait_ge(attn_high, b * QT + t + 1)
                dve.tensor_tensor(attn_t[:, LO], attn_bank[:].rearrange("p (g q) -> p g q", g=G), as_f32(attn_t[:, HI]),
                                  ALU.subtract).then_inc(attn_read, 1)

            def residual(b, t):
                dve.wait_ge(done["proj"], b * QT + t + 1)
                tile = x_tile(b, t)
                dve.scalar_tensor_tensor(out=tile, in0=bank_of["proj", t][:], scalar=gates[:, 0:1], in1=tile,
                                         op0=ALU.mult, op1=ALU.add).then_inc(read["proj"], 1)
                dve.wait_ge(read["proj"], b * QT + t + 1)
                if not (isinstance(b, int) and b == 0 and t == 0):
                    dve.wait_ge(stats2_ready, b * QT + t)
                apart(dve)
                dve.bn_stats(stats2[:], tile).then_inc(stats2_part, 1)
                dve.wait_ge(stats2_part, b * QT + t + 1)
                if not (isinstance(b, int) and b == 0 and t == 0):
                    dve.wait_ge(var2_ready, b * QT + t)
                    dve.wait_ge(norm2_ready, b * QT + t)
                apart(dve)
                dve.bn_aggr(mv2[:], stats2[:]).then_inc(stats2_ready, 1)

            def normalise2(b, t):
                dve.wait_ge(rstd2_ready, b * QT + t + 1)
                if not (isinstance(b, int) and b == 0 and t < 2):
                    dve.wait_ge(done["turn2"], b * QT + t - 1)
                dve.tensor_scalar(norm2[:, t % 2], x_tile(b, t), mv2[:, 0:1], rstd2[:], ALU.subtract, ALU.mult)\
                    .then_inc(norm2_ready, 1)

            def mix(b, t):
                dve.wait_ge(diff_ready, b * QT + t + 1)
                if not (isinstance(b, int) and b == 0 and t == 0):
                    dve.wait_ge(mixg_low, b * QT + t)
                for c in range(CT):
                    m = dve.scalar_tensor_tensor(out=mix_g[:, c, :], in0=diff[:, c, :], scalar=mu[:, 0, c:c + 1],
                                                 in1=xn2t[:, t % 2, c, 0:P], op0=ALU.mult, op1=ALU.add)
                m.then_inc(mixg_ready, 1)
                dve.wait_ge(mixg_ready, b * QT + t + 1)
                for c in range(CT):
                    m = dve.scalar_tensor_tensor(out=diff[:, c, :], in0=diff[:, c, :], scalar=mu[:, 1, c:c + 1],
                                                 in1=xn2t[:, t % 2, c, 0:P], op0=ALU.mult, op1=ALU.add)
                m.then_inc(mixk_ready, 1)

            def finish(b, t):
                dve.wait_ge(read["gate"], b * QT + t + 1)
                dve.wait_ge(done["value"], b * QT + t + 1)
                dve.scalar_tensor_tensor(out=gated[:, t % 2], in0=gated[:, t % 2], scalar=1.0, in1=bank_of["value", t][:],
                                         op0=ALU.add, op1=ALU.mult).then_inc(read["value"], 1)
                dve.wait_ge(read["value"], b * QT + t + 1)
                dve.scalar_tensor_tensor(out=gated[:, t % 2], in0=gated[:, t % 2], scalar=half_gate[:], in1=x_tile(b, t),
                                         op0=ALU.mult, op1=ALU.add).then_inc(out_ready, 1)

            def batch(b, ffn, last):
                f = sub(b, 1)
                for g in range(G):
                    bias(b, 0, g)
                reciprocals(b, 0, 0)
                bias(b, 1, 0)
                bias(b, 1, 1)
                reciprocals(b, 0, 1)
                bias(b, 1, 2)
                bias(b, 1, 3)
                reciprocals(b, 1, 0)
                attn_low(b, 0)
                if ffn:
                    finish(f, 0)
                for g in range(G):
                    bias(b, 2, g)
                reciprocals(b, 1, 1)
                residual(b, 0)
                attn_low(b, 1)
                if ffn:
                    finish(f, 1)
                bias(b, 3, 0)
                bias(b, 3, 1)
                normalise2(b, 0)
                reciprocals(b, 2, 0)
                reciprocals(b, 2, 1)
                bias(b, 3, 2)
                bias(b, 3, 3)
                residual(b, 1)
                attn_low(b, 2)
                if ffn:
                    finish(f, 2)
                reciprocals(b, 3, 0)
                mix(b, 0)
                reciprocals(b, 3, 1)
                normalise2(b, 1)
                residual(b, 2)
                attn_low(b, 3)
                if ffn:
                    finish(f, 3)
                if not last:
                    statistics1(b + 1)
                    normalise1(b + 1, 0)
                    turn1_low(b + 1, 0)
                    normalise1(b + 1, 1)
                    turn1_low(b + 1, 1)
                    normalise1(b + 1, 2)
                normalise2(b, 2)
                if not last:
                    turn1_low(b + 1, 2)
                    normalise1(b + 1, 3)
                    turn1_low(b + 1, 3)
                mix(b, 1)
                residual(b, 3)
                normalise2(b, 3)
                mix(b, 2)
                mix(b, 3)

            statistics1(0)
            for t in range(QT):
                normalise1(0, t)
                turn1_low(0, t)
            dve.wait_ge(gates_ready, 2)
            batch(0, False, False)
            with dve.Fori(1, NB - 1) as b:
                batch(b, True, False)
            batch(NB - 1, True, True)
            for t in range(QT):
                finish(NB - 1, t)

        @block.gpsimd
        def _(pool):
            as_f32 = lambda ap: ap.bitcast(F32)
            pool.memset(ident[:], 0.0).then_inc(ident_zero, 1)
            pool.memset(power[:], -0.5).then_inc(ident_zero, 1)
            pool.wait_ge(ident_zero, 2)
            pool.affine_select(out=ident[:], in_=ident[:], compare_op=ALU.not_equal, fill=1.0, base=0,
                               pattern=[[-1, P]], channel_multiplier=1).then_inc(consts_ready, 1)

            def distances(b):
                pool.wait_ge(mask_loaded, b * 32 + 32)
                if not (isinstance(b, int) and b == 0):
                    pool.wait_ge(scores_biased, b * QT * G)
                apart(pool)
                pool.tensor_scalar(neg_dist[:], mask_in[:], 0.0, BIG, ALU.is_equal, ALU.mult).then_inc(dist_mask, 1)
                apart(pool)
                pool.tensor_copy(kpos_f[:], kpos_in[:]).then_inc(dist_mask, 1)
                pool.wait_ge(dist_mask, b * 2 + 2)
                for t in range(QT):
                    m = pool.tensor_tensor(neg_dist[:, t], kpos_f[:], neg_dist[:, t], ALU.subtract)
                m.then_inc(dist_plain, 1)
                pool.wait_ge(dist_plain, b + 1)
                m = pool.tensor_tensor(neg_dist[:], neg_dist[:],
                                       qpos_f[:, bass.ds(b, 1), :].rearrange("p b t -> p (b t)").unsqueeze(2).to_broadcast((P, QT, NK)), ALU.subtract)
                m.then_inc(dist_ready, 1)

            def rstd1_of(b):
                pool.wait_ge(stats1_ready, (b + 1) * QT)
                apart(pool)
                pool.tensor_scalar(rstd1[:], mv1[:, :, 1], EPS, None, ALU.add).then_inc(var1_ready, 1)
                pool.wait_ge(var1_ready, b + 1)
                pool.tensor_tensor(rstd1[:], rstd1[:], power[:], ALU.pow).then_inc(rstd1_ready, 1)

            def rstd2_of(b, t):
                pool.wait_ge(stats2_ready, b * QT + t + 1)
                apart(pool)
                pool.tensor_scalar(rstd2[:], mv2[:, 1:2], EPS, None, ALU.add).then_inc(var2_ready, 1)
                pool.wait_ge(var2_ready, b * QT + t + 1)
                pool.tensor_tensor(rstd2[:], rstd2[:], power[:, 0:1], ALU.pow).then_inc(rstd2_ready, 1)

            def normalise_probs(b, t, half):
                heads = slice(half * H // 2, (half + 1) * H // 2)
                pool.wait_ge(recip_ready, (b * QT + t) * 2 + half + 1)
                part = probs[:, t % 2, heads, :]
                pool.tensor_tensor(part, part, recip[:, t % 2, heads].unsqueeze(2).to_broadcast((P, H // 2, NK)), ALU.mult)\
                    .then_inc(probs_ready, 1)

            def difference(b, t):
                pool.wait_ge(read["turn2"], b * QT + t + 1)
                if t > 0:
                    apart(pool)
                    pool.tensor_copy(xn2t[:, t % 2, :, 0:1], xn2t[:, (t - 1) % 2, :, P:P + 1]).then_inc(edge_ready, 1)
                elif not (isinstance(b, int) and b == 0):
                    apart(pool)
                    pool.memset(xn2t[:, 0, :, 0:1], 0.0).then_inc(edge_ready, 1)
                pool.wait_ge(edge_ready, b * QT + t + 1)
                if not (isinstance(b, int) and b == 0 and t == 0):
                    pool.wait_ge(mixk_low, b * QT + t)
                pool.tensor_tensor(diff[:], xn2t[:, t % 2, :, 1:], xn2t[:, t % 2, :, 0:P], ALU.subtract)\
                    .then_inc(diff_ready, 1)

            def mix_low(b, t):
                tokens = slice(t * P, (t + 1) * P)
                pool.wait_ge(mixg_high, b * QT + t + 1)
                pool.tensor_tensor(mixed_gate[:, LO, :, tokens], mix_g[:], as_f32(mixed_gate[:, HI, :, tokens]),
                                   ALU.subtract).then_inc(mixg_low, 1)
                pool.wait_ge(mixk_high, b * QT + t + 1)
                pool.tensor_tensor(mixed_key[:, LO, :, tokens], diff[:], as_f32(mixed_key[:, HI, :, tokens]),
                                   ALU.subtract).then_inc(mixk_low, 1)

            def squared_relu(b, m):
                pool.wait_ge(read["key"], b * CT + m + 1)
                if m > 0:
                    pool.wait_ge(act_low, b * CT + m)
                pool.tensor_tensor(square[:], relu[:], relu[:], ALU.mult).then_inc(square_ready, 1)
                pool.wait_ge(act_high, b * CT + m + 1)
                pool.tensor_tensor(xnt_or_act[:, LO, m, :], square[:], as_f32(xnt_or_act[:, HI, m, :]),
                                   ALU.subtract).then_inc(act_low, 1)

            def batch(b, ffn, last):
                f = sub(b, 1)
                if ffn:
                    for m in range(CT):
                        squared_relu(f, m)
                for t in range(3):
                    normalise_probs(b, t, 0)
                    normalise_probs(b, t, 1)
                    if t >= 1:
                        rstd2_of(b, t - 1)
                difference(b, 0)
                mix_low(b, 0)
                normalise_probs(b, 3, 0)
                normalise_probs(b, 3, 1)
                if not last:
                    distances(b + 1)
                    rstd1_of(b + 1)
                rstd2_of(b, 2)
                difference(b, 1)
                mix_low(b, 1)
                rstd2_of(b, 3)
                difference(b, 2)
                mix_low(b, 2)
                difference(b, 3)
                mix_low(b, 3)

            pool.wait_ge(consts_ready, 2)
            rstd1_of(0)
            distances(0)
            batch(0, False, False)
            with pool.Fori(1, NB - 1) as b:
                batch(b, True, False)
            batch(NB - 1, True, True)
            for m in range(CT):
                squared_relu(NB - 1, m)


def kernel(x, ctx_1024, itok_BxS_8_8191, itok_BxS2_1_8191, mask_BxSxS2_if1, g_xattn, g_ffn,
           L0_xattn_W_q, L0_xattn_W_k, L0_xattn_W_v, L0_xattn_W_o, L0_ffn_W_r, L0_ffn_W_k, L0_ffn_W_v,
           L0_ffn_mu_r, L0_ffn_mu_k):
    import concourse.bacc as bacc
    from concourse.bass_utils import run_bass_kernel_spmd

    per_partition = lambda a: np.asarray(a).reshape(-1, P).T
    arrays = {
        "x": x, "ctx_t": np.asarray(ctx_1024).reshape(-1, np.asarray(ctx_1024).shape[-1]).T,
        "qpos": per_partition(itok_BxS_8_8191), "kpos": itok_BxS2_1_8191, "mask": mask_BxSxS2_if1,
        "g_xattn": g_xattn, "g_ffn": g_ffn,
        "wq": np.asarray(L0_xattn_W_q).T, "wk": np.asarray(L0_xattn_W_k).T, "wv": np.asarray(L0_xattn_W_v).T,
        "wo": np.asarray(L0_xattn_W_o).T, "ffn_wr": np.asarray(L0_ffn_W_r).T, "ffn_wk": np.asarray(L0_ffn_W_k).T,
        "ffn_wv": np.asarray(L0_ffn_W_v).T, "mu_r": per_partition(L0_ffn_mu_r), "mu_k": per_partition(L0_ffn_mu_k),
    }
    nc = bacc.Bacc("TRN2", target_bir_lowering=False, num_devices=1)
    feeds, args = {}, []
    for name, a in arrays.items():
        a = np.ascontiguousarray(a)
        feeds[f"in_{name}_dram"] = a
        args.append(nc.dram_tensor(f"in_{name}_dram", a.shape, mybir.dt.from_np(a.dtype), kind="ExternalInput").ap())
    out = nc.dram_tensor("out_dram", x.shape, F32, kind="ExternalOutput").ap()
    flamingo_block(nc, *args, out)
    result = run_bass_kernel_spmd(nc, [feeds], core_ids=[0])
    return result.results[0]["out_dram"]
```

```python
from contextlib import ExitStack

import numpy as np

import concourse.bass as bass
from concourse import mybir

F32 = mybir.dt.float32
F32R = mybir.dt.float32r
I32 = mybir.dt.int32
ALU = mybir.AluOpType
ACT = mybir.ActivationFunctionType
AX = mybir.AxisListType

P = 128
HI, LO = 0, 1

SPLIT_PASSES = ((HI, HI), (HI, LO), (LO, HI))

ATTENTION_AND_FFN = (
    ("key", 0, -1), ("key", 1, -1), ("key", 2, -1), ("key", 3, -1), ("gate", 0, -1), ("gate", 1, -1),
    ("value", 0, -1), ("proj", 0, 0), ("value", 1, -1), ("gate", 2, -1), ("turn2", 0, 0), ("proj", 1, 0),
    ("value", 2, -1), ("gate", 3, -1), ("value", 3, -1), ("turn2", 1, 0), ("proj", 2, 0),
    ("turn1", 0, 1), ("turn1", 1, 1), ("proj", 3, 0), ("turn1", 2, 1), ("turn2", 2, 0), ("turn1", 3, 1),
    ("query", 0, 1), ("turn2", 3, 0), ("query", 1, 1), ("query", 2, 1), ("query", 3, 1),
)


def flamingo_block(nc, x, ctx_t, qpos, kpos, mask, g_xattn, g_ffn, wq, wk, wv, wo,
                   ffn_wr, ffn_wk, ffn_wv, mu_r, mu_k, out):
    NB, S, D = x.shape
    NK = kpos.shape[1]
    H = 16
    HD = D // H
    QT = S // P
    CT = D // P
    G = CT
    J = P // HD
    CB = 2
    CK = CB * NK
    EPS = 1e-5
    BIG = 1e30
    SCALE = 1.0 / float(np.sqrt(HD))
    RATIO = 2.0 ** (-8.0 / H)
    SLOPES = [float(np.float32(RATIO ** i)) for i in range(1, H + 1)]
    assert S == 512 and D == 512 and NB % (2 * CB) == 0 and NB > 2

    key_scratch = nc.dram_tensor("key_scratch", (NB, P, CT, NK), F32, kind="Internal").ap()
    value_scratch = nc.dram_tensor("value_scratch", (NB, NK, D), F32, kind="Internal").ap()

    with ExitStack() as stack:
        def sb(name, shape, dt=F32):
            return stack.enter_context(nc.sbuf_tensor(name, shape, dt))

        def sem(name):
            return stack.enter_context(nc.semaphore(name))

        w_query, w_proj, w_gate, w_key, w_value = (
            sb(n, [P, 2, CT, D], F32R) for n in ("w_query", "w_proj", "w_gate", "w_key", "w_value"))
        xs = sb("xs", [P, 2, QT, D])
        norm1 = sb("norm1", [P, 2, D])
        norm2 = sb("norm2", [P, 2, D])
        xnt_or_act = sb("xnt_or_act", [P, 2, CT, S], F32R)
        mixed_key = sb("mixed_key", [P, 2, CT, S], F32R)
        mixed_gate = sb("mixed_gate", [P, 2, CT, S], F32R)
        xn2t = sb("xn2t", [P, 2, CT, 1 + P])
        diff = sb("diff", [P, CT, P])
        mix_k = sb("mix_k", [P, CT, P])
        query_t = sb("query_t", [P, CT, S])
        probs = sb("probs", [P, 2, H, NK])
        probs_t = sb("probs_t", [NK, 2, J, P])
        attn_t = sb("attn_t", [P, 2, G, P], F32R)
        keys_t = sb("keys_t", [P, CT, NK])
        values = sb("values", [NK, D])
        gated = sb("gated", [P, 2, D])
        relu = sb("relu", [P, S])
        square = sb("square", [P, S])
        mask_in = sb("mask_in", [P, QT, NK], I32)
        kpos_in = sb("kpos_in", [P, NK], I32)
        neg_dist = mask_in[:].bitcast(F32)
        qpos_in = sb("qpos_in", [P, NB, QT], I32)
        qpos_f = sb("qpos_f", [P, NB, QT])
        ident = sb("ident", [P, P])
        mu = sb("mu", [P, 2, CT])
        gates_in = sb("gates_in", [P, 2])
        gates = sb("gates", [P, 2])
        half_gate = sb("half_gate", [P, 1])
        stats1 = sb("stats1", [P, QT, 6])
        stats2 = sb("stats2", [P, 6])
        mv1 = sb("mv1", [P, QT, 2])
        rstd1 = sb("rstd1", [P, QT])
        mv2 = sb("mv2", [P, 2])
        rstd2 = sb("rstd2", [P, 1])
        power = sb("power", [P, 1])
        neg_max = sb("neg_max", [P, 2, H])
        sums = sb("sums", [P, 2, H])
        sums1 = sb("sums1", [P, 2, H])
        recip = sb("recip", [P, 2, H])

        wk_split = mixed_key
        wv_split = mixed_gate
        ctx_raw = probs[:].rearrange("p a h k -> p (a h k)").rearrange("p (a c k) -> p a c k", a=4, k=CK)
        ctx_split = [xnt_or_act[:].rearrange("p s c t -> p (s c t)")[:, i * 2 * CT * CK:(i + 1) * 2 * CT * CK]
                     .rearrange("p (s c k) -> p s c k", s=2, c=CT) for i in range(2)]
        key_out = query_t[:].rearrange("p c t -> p (c t)").rearrange("p (a c k) -> p a c k", a=2, c=CT)[:, :, :, 0:CK]
        value_out = gated

        score_banks = [stack.enter_context(nc.psum_tensor(f"score_bank{j}", [P, 512], F32)) for j in range(J)]
        rotating = [stack.enter_context(nc.psum_tensor(f"rotating{i}", [P, 512], F32)) for i in range(2)]
        probs_bank = stack.enter_context(nc.psum_tensor("probs_bank", [P, 512], F32))
        attn_bank = stack.enter_context(nc.psum_tensor("attn_bank", [P, 512], F32))
        bank_of = {(what, tile): rotating[i % 2] for i, (what, tile, _) in enumerate(ATTENTION_AND_FFN)}
        without_ffn = [u for u in ATTENTION_AND_FFN if u[2] >= 0]

        small_loaded = sem("small_loaded")
        raw_weight = [sem(f"raw_weight{i}") for i in range(2)]
        ctx_loaded = [sem(f"ctx_loaded{i}") for i in range(2)]
        x_loaded = [sem(f"x_loaded{t}") for t in range(QT)]
        mask_loaded = sem("mask_loaded")
        keys_loaded = sem("keys_loaded")
        values_loaded = sem("values_loaded")
        keys_stored = [sem(f"keys_stored{i}") for i in range(2)]
        gated_stored = [sem(f"gated_stored{i}") for i in range(2)]
        ident_zero = sem("ident_zero")
        consts_ready = sem("consts_ready")
        gates_ready = sem("gates_ready")
        weight_high = sem("weight_high")
        weight_low = sem("weight_low")
        ctx_high = sem("ctx_high")
        ctx_low = sem("ctx_low")
        kproj_done = sem("kproj_done")
        kproj_read = sem("kproj_read")
        vproj_done = sem("vproj_done")
        vproj_read = sem("vproj_read")
        done = {k: sem(f"{k}_done") for k in ("key", "gate", "value", "proj", "query", "turn1", "turn2")}
        read = {k: sem(f"{k}_read") for k in ("key", "gate", "value", "proj", "query", "turn1", "turn2")}
        turn1_high = sem("turn1_high")
        scores_done = sem("scores_done")
        scores_biased = sem("scores_biased")
        max_ready = sem("max_ready")
        exp_done = sem("exp_done")
        sum_ready = sem("sum_ready")
        recip_ready = sem("recip_ready")
        probs_ready = sem("probs_ready")
        probs_turned = sem("probs_turned")
        probs_t_ready = sem("probs_t_ready")
        attn_done = sem("attn_done")
        attn_high = sem("attn_high")
        attn_read = sem("attn_read")
        dist_mask = sem("dist_mask")
        dist_plain = sem("dist_plain")
        dist_ready = sem("dist_ready")
        stats1_part = sem("stats1_part")
        stats1_ready = sem("stats1_ready")
        var1_ready = sem("var1_ready")
        rstd1_ready = sem("rstd1_ready")
        norm1_ready = sem("norm1_ready")
        x2_ready = sem("x2_ready")
        stats2_part = sem("stats2_part")
        stats2_ready = sem("stats2_ready")
        var2_ready = sem("var2_ready")
        rstd2_ready = sem("rstd2_ready")
        norm2_ready = sem("norm2_ready")
        edge_ready = sem("edge_ready")
        diff_ready = sem("diff_ready")
        mixg_ready = sem("mixg_ready")
        mixk_ready = sem("mixk_ready")
        mixg_high = sem("mixg_high")
        mixk_high = sem("mixk_high")
        mixg_low = sem("mixg_low")
        mixk_low = sem("mixk_low")
        square_ready = sem("square_ready")
        act_high = sem("act_high")
        act_low = sem("act_low")
        gated_part = sem("gated_part")
        out_ready = sem("out_ready")

        raw = [wk, wv, wq, ffn_wk, ffn_wr, ffn_wv, wo]
        split = [wk_split, wv_split, w_query, w_key, w_gate, w_value, w_proj]
        NCHUNK = NB // CB

        def sub(b, k):
            return b - k

        def apart(engine):
            engine.nop(nofuse=True)

        block = stack.enter_context(nc.Block())

        @block.sync
        def _(sp):
            for dst, src in ((qpos_in[:].rearrange("p b t -> p (b t)"), qpos), (mu[:, 0, :], mu_r), (mu[:, 1, :], mu_k),
                             (gates_in[:, 0:1], g_xattn.rearrange("(a n) -> a n", a=1).to_broadcast((P, 1))),
                             (gates_in[:, 1:2], g_ffn.rearrange("(a n) -> a n", a=1).to_broadcast((P, 1)))):
                sp.dma_start(dst, src).then_inc(small_loaded, 16)

            def load_weight(i):
                if i >= 2:
                    sp.wait_ge(weight_low, i - 1)
                sp.dma_start(xs[:, i % 2], raw[i].rearrange("(c p) n -> p c n", p=P)).then_inc(raw_weight[i % 2], 16)

            def load_ctx(chunk, i, wait=None):
                if wait is not None:
                    sp.wait_ge(ctx_low, wait)
                sp.dma_start(ctx_raw[:, i], ctx_t[:, bass.ds(chunk * CK, CK)].rearrange("(c p) k -> p c k", p=P))\
                    .then_inc(ctx_loaded[i], 16)

            def store_chunk(n, i):
                sp.wait_ge(kproj_read, n * 2 * CT + (i + 1) * CT)
                for b in range(CB):
                    sp.dma_start(key_scratch[bass.ds((n * 2 + i) * CB + b, 1)].rearrange("b p c k -> p (b c) k"),
                                 key_out[:, i, :, b * NK:(b + 1) * NK]).then_inc(keys_stored[i], 16)
                for b in range(CB):
                    sp.wait_ge(vproj_read, n * 2 * CB + i * CB + b + 1)
                    sp.dma_start(value_scratch[bass.ds((n * 2 + i) * CB + b, 1)].rearrange("b k d -> (b k) d"),
                                 value_out[0:NK, b, :]).then_inc(gated_stored[b], 16)

            load_ctx(0, 0)
            load_weight(0)
            load_weight(1)
            load_ctx(1, 1)
            for i in range(2, len(raw)):
                load_weight(i)
            with sp.Fori(0, NCHUNK // 2 - 1) as n:
                for i in range(2):
                    load_ctx(n * 2 + 2 + i, i, wait=n * 2 + i + 1)
                    store_chunk(n, i)
            for i in range(2):
                store_chunk(NCHUNK // 2 - 1, i)
            for i in range(2):
                sp.wait_ge(keys_stored[i], 16 * CB * (NCHUNK // 2))
                sp.wait_ge(gated_stored[i], 16 * NCHUNK)

            def load_x(b, t):
                sp.dma_start(xs[:, bass.ds(b % 2, 1), t].rearrange("p a d -> p (a d)"),
                             x[bass.ds(b, 1), t * P:(t + 1) * P, :].rearrange("b p d -> (b p) d")).then_inc(x_loaded[t], 16)

            def load_mask(b):
                sp.dma_start(mask_in[:], mask[bass.ds(b, 1)].rearrange("b (t p) k -> p (b t) k", p=P))\
                    .then_inc(mask_loaded, 16)
                sp.dma_start(kpos_in[:], kpos[bass.ds(b, 1)].to_broadcast((P, NK))).then_inc(mask_loaded, 16)

            def load_keys(b):
                sp.dma_start(keys_t[:], key_scratch[bass.ds(b, 1)].rearrange("b p c k -> p (b c) k")).then_inc(keys_loaded, 16)

            def load_values(b):
                sp.dma_start(values[:], value_scratch[bass.ds(b, 1)].rearrange("b k d -> (b k) d"))\
                    .then_inc(values_loaded, 16)

            def store_out(b, t):
                sp.wait_ge(out_ready, b * QT + t + 1)
                sp.dma_start(out[bass.ds(b, 1), t * P:(t + 1) * P, :].rearrange("b p d -> (b p) d"),
                             gated[:, t % 2]).then_inc(gated_stored[t % 2], 16)

            sp.wait_ge(weight_low, len(raw))
            for t in range(QT):
                load_x(0, t)
            load_mask(0)
            load_keys(0)
            load_values(0)

            def batch(b, ffn, last):
                if not ffn:
                    sp.wait_ge(stats1_ready, QT)
                    for t in range(QT):
                        load_x(b + 1, t)
                for t in range(QT):
                    if ffn:
                        store_out(b - 1, t)
                        if not last:
                            load_x(b + 1, t)
                    if t == 1 and not last:
                        sp.wait_ge(scores_biased, (b + 1) * QT * G)
                        load_mask(b + 1)
                        load_keys(b + 1)
                if not last:
                    sp.wait_ge(attn_done, (b + 1) * QT)
                    load_values(b + 1)

            batch(0, False, False)
            with sp.Fori(1, NB - 1) as b:
                batch(b, True, False)
            batch(NB - 1, True, True)
            for t in range(QT):
                store_out(NB - 1, t)
            for i in range(2):
                sp.wait_ge(gated_stored[i], 16 * (NCHUNK + NB * QT // 2))

        @block.tensor
        def _(pe):
            def product(bank, stationary, moving, steps=range(CT)):
                mm = None
                for c in steps:
                    for n, (a, b) in enumerate(SPLIT_PASSES):
                        mm = pe.matmul(bank, stationary(a, c), moving(b, c), start=(c == 0 and n == 0),
                                       stop=(c == CT - 1 and n == len(SPLIT_PASSES) - 1))
                return mm

            pe.wait_ge(consts_ready, 1)

            def chunk(n, i, first):
                pe.wait_ge(ctx_low, n * 2 + i + 1)
                for m in range(CT):
                    if m < 2 and not first:
                        pe.wait_ge(vproj_read, n * 2 * CB + i * CB - CB + m + 1)
                    if m >= 2:
                        pe.wait_ge(kproj_read, n * 2 * CT + i * CT + m - 1)
                    product(rotating[m % 2][:, 0:CK], lambda s, c: wk_split[:, s, c, m * P:(m + 1) * P],
                            lambda s, c: ctx_split[i][:, s, c, :]).then_inc(kproj_done, 1)
                if first:
                    pe.wait_ge(weight_low, 2)
                for b in range(CB):
                    pe.wait_ge(kproj_read, n * 2 * CT + i * CT + 3 + b)
                    product(rotating[b][0:NK, :], lambda s, c: ctx_split[i][:, s, c, b * NK:(b + 1) * NK],
                            lambda s, c: wv_split[:, s, c, :]).then_inc(vproj_done, 1)

            pe.wait_ge(weight_low, 1)
            chunk(0, 0, True)
            chunk(0, 1, False)
            with pe.Fori(1, NCHUNK // 2) as n:
                chunk(n, 0, False)
                chunk(n, 1, False)

            def free_bank(b, use, order, before):
                same = [u for u in before + order if bank_of[u[0], u[1]] is bank_of[use[0], use[1]]]
                own = len([u for u in before if u in same])
                at = own + [u for u in order if u in same].index(use)
                if at == 0:
                    return
                what, tile, rel = same[at - 1]
                if at - 1 < own:
                    rel -= 1
                pe.wait_ge(read[what], (b + rel) * 4 + tile + 1)

            def scores(b, t, g):
                if t == 0:
                    pe.wait_ge(read["query"], b * CT + g + 1)
                    if g == 0:
                        pe.wait_ge(keys_loaded, b * 16 + 16)
                if g == 0 and not (isinstance(b, int) and b == 0 and t == 0):
                    pe.wait_ge(scores_biased, (b * QT + t) * G)
                for j in range(J):
                    rows = slice(j * HD, (j + 1) * HD)
                    mm = pe.matmul(score_banks[j][:, g * NK:(g + 1) * NK], query_t[rows, g, t * P:(t + 1) * P],
                                   keys_t[rows, g, :], start=True, stop=True)
                if g == G - 1:
                    mm.then_inc(scores_done, 1)

            def turn1(b, t, steps):
                pe.wait_ge(norm1_ready, b * QT + t + 1)
                for c in range(CT):
                    mm = pe.transpose(bank_of["turn1", t][:, c * P:(c + 1) * P], norm1[:, t % 2, c * P:(c + 1) * P], ident[:])
                return mm

            def turn2(b, t, steps):
                pe.wait_ge(norm2_ready, b * QT + t + 1)
                for c in range(CT):
                    mm = pe.transpose(bank_of["turn2", t][:, c * P:(c + 1) * P], norm2[:, t % 2, c * P:(c + 1) * P], ident[:])
                return mm

            def query(b, m, steps):
                if m == 0:
                    pe.wait_ge(read["turn1"], (b + 1) * QT)
                return product(bank_of["query", m][:], lambda s, c: w_query[:, s, c, m * P:(m + 1) * P],
                               lambda s, c: xnt_or_act[:, s, c, :], steps)

            def key(b, m, steps):
                if m == 0 and steps[0] == 0:
                    pe.wait_ge(mixk_low, (b + 1) * QT)
                return product(bank_of["key", m][:], lambda s, c: w_key[:, s, c, m * P:(m + 1) * P],
                               lambda s, c: mixed_key[:, s, c, :], steps)

            def gate(b, t, steps):
                if t == 0 and steps[0] == 0:
                    pe.wait_ge(mixg_low, (b + 1) * QT)
                return product(bank_of["gate", t][:], lambda s, c: mixed_gate[:, s, c, t * P:(t + 1) * P],
                               lambda s, c: w_gate[:, s, c, :], steps)

            def value(b, t, steps):
                if t == 0 and steps[0] == 0:
                    pe.wait_ge(act_low, (b + 1) * CT)
                return product(bank_of["value", t][:], lambda s, c: xnt_or_act[:, s, c, t * P:(t + 1) * P],
                               lambda s, c: w_value[:, s, c, :], steps)

            def proj(b, t, steps):
                if steps[0] == 0:
                    pe.wait_ge(attn_read, b * QT + t + 1)
                return product(bank_of["proj", t][:], lambda s, c: attn_t[:, s, c, :],
                               lambda s, c: w_proj[:, s, c, :], steps)

            made = {"key": key, "gate": gate, "value": value, "proj": proj, "turn1": turn1, "turn2": turn2, "query": query}

            def turn_probs(b, t, g):
                pe.wait_ge(probs_ready, (b * QT + t) * 2 + g // 2 + 1)
                if not (isinstance(b, int) and b == 0 and t == 0 and g == 0):
                    pe.wait_ge(probs_t_ready, (b * QT + t) * G + g)
                for j in range(J):
                    mm = pe.transpose(probs_bank[0:NK, j * P:(j + 1) * P], probs[:, t % 2, g * J + j, :], ident[:])
                mm.then_inc(probs_turned, 1)

            def attend(b, t, g):
                pe.wait_ge(probs_t_ready, (b * QT + t) * G + g + 1)
                if g == 0:
                    if t == 0:
                        pe.wait_ge(values_loaded, b * 16 + 16)
                    if not (isinstance(b, int) and b == 0 and t == 0):
                        pe.wait_ge(attn_read, b * QT + t)
                for j in range(J):
                    head = g * J + j
                    mm = pe.matmul(attn_bank[j * HD:(j + 1) * HD, g * P:(g + 1) * P],
                                   values[:, head * HD:(head + 1) * HD], probs_t[:, g % 2, j, :],
                                   start=True, stop=True, skip_group_check=True)
                if g == G - 1:
                    mm.then_inc(attn_done, 1)

            def batch(b, ffn, last, before):
                order = [u for u in ATTENTION_AND_FFN if (ffn or u[2] >= 0) and (not last or u[2] <= 0)]

                def use(what, tile, steps=range(CT)):
                    found = [u for u in order if u[:2] == (what, tile)]
                    if not found:
                        return
                    if steps[0] == 0:
                        free_bank(b, found[0], order, before)
                    mm = made[what](b + found[0][2], tile, steps)
                    if steps[-1] == CT - 1:
                        mm.then_inc(done[what], 1)

                def with_scores(t, what, tile):
                    for g in range(G):
                        scores(b, t, g)
                        use(what, tile, [g])

                def with_attention(t, what, tile):
                    for g in range(G):
                        turn_probs(b, t, g)
                        use(what, tile, [g])
                        if g > 0:
                            attend(b, t, g - 1)
                    attend(b, t, G - 1)

                with_scores(0, "key", 0)
                use("key", 1)
                use("key", 2)
                with_scores(1, "key", 3)
                with_attention(0, "gate", 0)
                use("gate", 1)
                with_scores(2, "value", 0)
                use("proj", 0)
                with_attention(1, "value", 1)
                with_scores(3, "gate", 2)
                use("turn2", 0)
                use("proj", 1)
                with_attention(2, "value", 2)
                use("gate", 3)
                use("value", 3)
                use("turn2", 1)
                with_attention(3, "proj", 2)
                use("turn1", 0)
                use("turn1", 1)
                use("proj", 3)
                use("turn1", 2)
                use("turn2", 2)
                use("turn1", 3)
                use("query", 0)
                use("turn2", 3)
                use("query", 1)
                use("query", 2)
                use("query", 3)

            pe.wait_ge(vproj_read, NB)
            pe.wait_ge(kproj_read, NCHUNK * CT)
            first = [u for u in ATTENTION_AND_FFN if u[0] in ("turn1", "query")]
            for u in first:
                free_bank(-1, u, first, [])
                made[u[0]](0, u[1], range(CT)).then_inc(done[u[0]], 1)
            batch(0, False, False, first)
            full = list(ATTENTION_AND_FFN)
            with pe.Fori(1, NB - 1) as b:
                batch(b, True, False, full)
            batch(NB - 1, True, True, full)
            last_uses = [u for u in ATTENTION_AND_FFN if u[2] < 0]
            before = [u for u in ATTENTION_AND_FFN if u[2] <= 0]
            for u in last_uses:
                free_bank(NB, u, last_uses, before)
                made[u[0]](NB - 1, u[1], range(CT)).then_inc(done[u[0]], 1)

        @block.scalar
        def _(act):
            act.wait_ge(small_loaded, 16 * 5)
            act.activation(gates[:], gates_in[:], ACT.Tanh).then_inc(gates_ready, 1)
            act.wait_ge(gates_ready, 1)
            act.mul(half_gate[:], gates[:, 1:2], 0.5).then_inc(gates_ready, 1)

            def weight(i):
                act.wait_ge(raw_weight[i % 2], 16 * (i // 2 + 1))
                act.copy(split[i][:, HI], xs[:, i % 2]).then_inc(weight_high, 1)

            def chunk(n, i, first, extra=None):
                act.wait_ge(ctx_loaded[i], 16 * n + 16)
                if not first:
                    act.wait_ge(vproj_done, n * 2 * CB + i * CB - CB)
                act.copy(ctx_split[i][:, HI], ctx_raw[:, i]).then_inc(ctx_high, 1)

            def keys_out(n, i, first):
                if not first:
                    act.wait_ge(keys_stored[i], 16 * CB * n)
                for m in range(CT):
                    act.wait_ge(kproj_done, n * 2 * CT + i * CT + m + 1)
                    act.copy(key_out[:, i, m, :], rotating[m % 2][:, 0:CK]).then_inc(kproj_read, 1)

            weight(0)
            chunk(0, 0, True)
            weight(1)
            chunk(0, 1, True)
            weight(2)
            keys_out(0, 0, True)
            weight(3)
            weight(4)
            keys_out(0, 1, True)
            weight(5)
            weight(6)
            with act.Fori(1, NCHUNK // 2) as n:
                for i in range(2):
                    chunk(n, i, False)
                    keys_out(n, i, False)

            def turn1_out(b, t):
                if t == 0 and not (isinstance(b, int) and b < 2):
                    act.wait_ge(done["value"], (b - 1) * QT)
                act.wait_ge(done["turn1"], b * QT + t + 1)
                act.copy(xnt_or_act[:, HI, :, t * P:(t + 1) * P],
                         bank_of["turn1", t][:].rearrange("p (c q) -> p c q", c=CT)).then_inc(turn1_high, 1)

            def query_out(b, m):
                act.wait_ge(done["query"], b * CT + m + 1)
                act.mul(query_t[:, m, :], bank_of["query", m][:], SCALE).then_inc(read["query"], 1)

            def exps(b, t, g):
                act.wait_ge(max_ready, (b * QT + t) * G + g + 1)
                for j in range(J):
                    head = g * J + j
                    e = act.activation(probs[:, t % 2, head, :], probs[:, t % 2, head, :], ACT.Exp,
                                       bias=neg_max[:, t % 2, head:head + 1],
                                       accum_out=sums[:, t % 2, head:head + 1])
                e.then_inc(exp_done, 1)

            def probs_out(b, t, g):
                act.wait_ge(probs_turned, (b * QT + t) * G + g + 1)
                act.copy(probs_t[:, g % 2], probs_bank[0:NK, :].rearrange("k (j q) -> k j q", j=J))\
                    .then_inc(probs_t_ready, 1)

            def attn_out(b, t):
                act.wait_ge(attn_done, b * QT + t + 1)
                if not (isinstance(b, int) and b == 0 and t == 0):
                    act.wait_ge(done["proj"], b * QT + t)
                act.copy(attn_t[:, HI], attn_bank[:].rearrange("p (g q) -> p g q", g=G)).then_inc(attn_high, 1)

            def turn2_out(b, t):
                act.wait_ge(done["turn2"], b * QT + t + 1)
                if t > 0:
                    act.wait_ge(edge_ready, b * QT + t)
                if not (isinstance(b, int) and b == 0 and t < 2):
                    act.wait_ge(mixg_ready, b * QT + t - 1)
                act.copy(xn2t[:, t % 2, :, 1:], bank_of["turn2", t][:].rearrange("p (c q) -> p c q", c=CT))\
                    .then_inc(read["turn2"], 1)

            def mix_high(b, t):
                act.wait_ge(mixk_ready, b * QT + t + 1)
                act.copy(mixed_key[:, HI, :, t * P:(t + 1) * P], mix_k[:]).then_inc(mixk_high, 1)
                act.wait_ge(mixg_ready, b * QT + t + 1)
                act.copy(mixed_gate[:, HI, :, t * P:(t + 1) * P], diff[:]).then_inc(mixg_high, 1)

            def relu_out(b, m):
                act.wait_ge(done["key"], b * CT + m + 1)
                act.activation(relu[:], bank_of["key", m][:], ACT.Relu).then_inc(read["key"], 1)

            def act_split(b, m):
                act.wait_ge(square_ready, b * CT + m + 1)
                act.copy(xnt_or_act[:, HI, m, :], square[:]).then_inc(act_high, 1)

            def gate_out(b, t):
                act.wait_ge(done["gate"], b * QT + t + 1)
                act.wait_ge(gated_stored[t % 2], (NCHUNK + b * 2 + t // 2) * 16)
                act.activation(gated[:, t % 2], bank_of["gate", t][:], ACT.Tanh, scale=0.5).then_inc(read["gate"], 1)

            def batch(b, ffn, last):
                f = sub(b, 1)

                def feed_forward(*steps):
                    if ffn:
                        for step, n in steps:
                            step(f, n)

                def after(*steps):
                    if not last:
                        for step, n in steps:
                            step(b + 1, n)

                feed_forward((relu_out, 0), (act_split, 0))
                exps(b, 0, 0)
                feed_forward((relu_out, 1))
                exps(b, 0, 1)
                feed_forward((act_split, 1), (relu_out, 2))
                exps(b, 0, 2)
                exps(b, 0, 3)
                feed_forward((act_split, 2), (relu_out, 3))
                probs_out(b, 0, 0)
                probs_out(b, 0, 1)
                feed_forward((act_split, 3))
                probs_out(b, 0, 2)
                probs_out(b, 0, 3)
                attn_out(b, 0)
                feed_forward((gate_out, 0))
                exps(b, 1, 0)
                exps(b, 1, 1)
                feed_forward((gate_out, 1))
                exps(b, 1, 2)
                exps(b, 1, 3)
                for g in range(G):
                    probs_out(b, 1, g)
                attn_out(b, 1)
                for g in range(G):
                    exps(b, 2, g)
                feed_forward((gate_out, 2))
                turn2_out(b, 0)
                exps(b, 3, 0)
                for g in range(G):
                    probs_out(b, 2, g)
                attn_out(b, 2)
                exps(b, 3, 1)
                exps(b, 3, 2)
                feed_forward((gate_out, 3))
                exps(b, 3, 3)
                mix_high(b, 0)
                turn2_out(b, 1)
                for g in range(G):
                    probs_out(b, 3, g)
                attn_out(b, 3)
                after((turn1_out, 0), (turn1_out, 1), (turn1_out, 2))
                turn2_out(b, 2)
                after((turn1_out, 3))
                mix_high(b, 1)
                after((query_out, 0))
                turn2_out(b, 3)
                mix_high(b, 2)
                after((query_out, 1), (query_out, 2))
                mix_high(b, 3)
                after((query_out, 3))

            for i in range(2):
                act.wait_ge(keys_stored[i], 16 * CB * (NCHUNK // 2))
                act.wait_ge(gated_stored[i], 16 * NCHUNK)
            act.wait_ge(vproj_done, NB)
            for t in range(QT):
                turn1_out(0, t)
            for m in range(CT):
                query_out(0, m)
            batch(0, False, False)
            with act.Fori(1, NB - 1) as b:
                batch(b, True, False)
            batch(NB - 1, True, True)
            for m in range(CT):
                relu_out(NB - 1, m)
                act_split(NB - 1, m)
            for t in range(QT):
                gate_out(NB - 1, t)

        @block.vector
        def _(dve):
            as_f32 = lambda ap: ap.bitcast(F32)
            dve.wait_ge(small_loaded, 16 * 5)
            dve.tensor_copy(qpos_f[:], qpos_in[:]).then_inc(consts_ready, 1)
            dve.memset(xn2t[:, 0, :, 0:1], 0.0).then_inc(edge_ready, 1)

            def weight(i):
                dve.wait_ge(weight_high, i + 1)
                dve.tensor_tensor(split[i][:, LO], xs[:, i % 2], as_f32(split[i][:, HI]), ALU.subtract)\
                    .then_inc(weight_low, 1)

            def chunk(n, i):
                dve.wait_ge(ctx_high, n * 2 + i + 1)
                dve.tensor_tensor(ctx_split[i][:, LO], ctx_raw[:, i], as_f32(ctx_split[i][:, HI]), ALU.subtract)\
                    .then_inc(ctx_low, 1)

            def values_out(n, i, first):
                for b in range(CB):
                    dve.wait_ge(vproj_done, n * 2 * CB + i * CB + b + 1)
                    if not first:
                        dve.wait_ge(gated_stored[b], (n * 2 + i) * 16)
                    dve.tensor_copy(value_out[0:NK, b, :], rotating[b][0:NK, :]).then_inc(vproj_read, 1)

            weight(0)
            chunk(0, 0)
            weight(1)
            chunk(0, 1)
            weight(2)
            values_out(0, 0, True)
            weight(3)
            weight(4)
            values_out(0, 1, False)
            weight(5)
            weight(6)
            with dve.Fori(1, NCHUNK // 2) as n:
                for i in range(2):
                    chunk(n, i)
                    values_out(n, i, False)

            def x_tile(b, t):
                return xs[:, bass.ds(b % 2, 1), t].rearrange("p a d -> p (a d)")

            def statistics1(b, t):
                dve.wait_ge(x_loaded[t], b * 16 + 16)
                if not (isinstance(b, int) and b == 0):
                    dve.wait_ge(stats1_ready, (b - 1) * QT + t + 1)
                    dve.wait_ge(norm1_ready, (b - 1) * QT + t + 1)
                apart(dve)
                dve.bn_stats(stats1[:, t, :], x_tile(b, t)).then_inc(stats1_part, 1)
                dve.wait_ge(stats1_part, b * QT + t + 1)
                apart(dve)
                dve.bn_aggr(mv1[:, t, :], stats1[:, t, :]).then_inc(stats1_ready, 1)

            def normalise1(b, t):
                dve.wait_ge(rstd1_ready, b * QT + t + 1)
                if not (isinstance(b, int) and b == 0 and t < 2):
                    dve.wait_ge(done["turn1"], b * QT + t - 1)
                dve.tensor_scalar(norm1[:, t % 2], x_tile(b, t), mv1[:, t, 0:1], rstd1[:, t:t + 1], ALU.subtract, ALU.mult)\
                    .then_inc(norm1_ready, 1)

            def turn1_low(b, t):
                dve.wait_ge(turn1_high, b * QT + t + 1)
                part = xnt_or_act[:, :, :, t * P:(t + 1) * P]
                dve.tensor_tensor(part[:, LO], bank_of["turn1", t][:].rearrange("p (c q) -> p c q", c=CT),
                                  as_f32(part[:, HI]), ALU.subtract).then_inc(read["turn1"], 1)

            def bias(b, t, g):
                if g == 0:
                    dve.wait_ge(scores_done, b * QT + t + 1)
                    if t == 0:
                        dve.wait_ge(dist_ready, b + 1)
                    if not (isinstance(b, int) and b == 0 and t < 2):
                        dve.wait_ge(probs_turned, (b * QT + t - 1) * G)
                        dve.wait_ge(exp_done, (b * QT + t - 1) * G)
                for j in range(J):
                    head = g * J + j
                    z = dve.scalar_tensor_tensor(out=probs[:, t % 2, head, :], in0=neg_dist[:, t, :], scalar=SLOPES[head],
                                                 in1=score_banks[j][:, g * NK:(g + 1) * NK], op0=ALU.mult, op1=ALU.add)
                z.then_inc(scores_biased, 1)
                dve.wait_ge(scores_biased, (b * QT + t) * G + g + 1)
                dve.tensor_reduce(neg_max[:, t % 2, g * J:(g + 1) * J], probs[:, t % 2, g * J:(g + 1) * J, :],
                                  AX.X, ALU.max, negate=True).then_inc(max_ready, 1)

            def reciprocals(b, t, half):
                heads = slice(half * H // 2, (half + 1) * H // 2)
                at = (b * QT + t) * 2 + half + 1
                dve.wait_ge(exp_done, (b * QT + t) * G + half * 2 + 2)
                if half == 0 and not (isinstance(b, int) and b == 0 and t < 2):
                    dve.wait_ge(probs_ready, (b * QT + t - 1) * 2)
                dve.tensor_scalar(sums1[:, t % 2, heads], sums[:, t % 2, heads], 1.0, None, ALU.add).then_inc(sum_ready, 1)
                dve.wait_ge(sum_ready, at)
                dve.reciprocal(recip[:, t % 2, heads], sums1[:, t % 2, heads]).then_inc(recip_ready, 1)

            def attn_low(b, t):
                dve.wait_ge(attn_high, b * QT + t + 1)
                dve.tensor_tensor(attn_t[:, LO], attn_bank[:].rearrange("p (g q) -> p g q", g=G), as_f32(attn_t[:, HI]),
                                  ALU.subtract).then_inc(attn_read, 1)

            def residual(b, t):
                dve.wait_ge(done["proj"], b * QT + t + 1)
                tile = x_tile(b, t)
                dve.scalar_tensor_tensor(out=tile, in0=bank_of["proj", t][:], scalar=gates[:, 0:1], in1=tile,
                                         op0=ALU.mult, op1=ALU.add).then_inc(read["proj"], 1)

            def statistics2(b, t):
                tile = x_tile(b, t)
                dve.wait_ge(read["proj"], b * QT + t + 1)
                if not (isinstance(b, int) and b == 0 and t == 0):
                    dve.wait_ge(stats2_ready, b * QT + t)
                apart(dve)
                dve.bn_stats(stats2[:], tile).then_inc(stats2_part, 1)
                dve.wait_ge(stats2_part, b * QT + t + 1)
                if not (isinstance(b, int) and b == 0 and t == 0):
                    dve.wait_ge(var2_ready, b * QT + t)
                    dve.wait_ge(norm2_ready, b * QT + t)
                apart(dve)
                dve.bn_aggr(mv2[:], stats2[:]).then_inc(stats2_ready, 1)

            def normalise2(b, t):
                dve.wait_ge(rstd2_ready, b * QT + t + 1)
                if not (isinstance(b, int) and b == 0 and t < 2):
                    dve.wait_ge(done["turn2"], b * QT + t - 1)
                dve.tensor_scalar(norm2[:, t % 2], x_tile(b, t), mv2[:, 0:1], rstd2[:], ALU.subtract, ALU.mult)\
                    .then_inc(norm2_ready, 1)

            def mix(b, t):
                dve.wait_ge(diff_ready, b * QT + t + 1)
                if not (isinstance(b, int) and b == 0 and t == 0):
                    dve.wait_ge(mixk_low, b * QT + t)
                for c in range(CT):
                    m = dve.scalar_tensor_tensor(out=mix_k[:, c, :], in0=diff[:, c, :], scalar=mu[:, 1, c:c + 1],
                                                 in1=xn2t[:, t % 2, c, 0:P], op0=ALU.mult, op1=ALU.add)
                m.then_inc(mixk_ready, 1)
                dve.wait_ge(mixk_ready, b * QT + t + 1)
                for c in range(CT):
                    m = dve.scalar_tensor_tensor(out=diff[:, c, :], in0=diff[:, c, :], scalar=mu[:, 0, c:c + 1],
                                                 in1=xn2t[:, t % 2, c, 0:P], op0=ALU.mult, op1=ALU.add)
                m.then_inc(mixg_ready, 1)

            def finish(b, t):
                dve.wait_ge(read["gate"], b * QT + t + 1)
                dve.wait_ge(done["value"], b * QT + t + 1)
                dve.scalar_tensor_tensor(out=gated[:, t % 2], in0=gated[:, t % 2], scalar=1.0, in1=bank_of["value", t][:],
                                         op0=ALU.add, op1=ALU.mult).then_inc(read["value"], 1)
                dve.wait_ge(read["value"], b * QT + t + 1)
                dve.scalar_tensor_tensor(out=gated[:, t % 2], in0=gated[:, t % 2], scalar=half_gate[:], in1=x_tile(b, t),
                                         op0=ALU.mult, op1=ALU.add).then_inc(out_ready, 1)

            def distances(b):
                dve.wait_ge(mask_loaded, b * 32 + 32)
                dve.tensor_scalar(neg_dist, mask_in[:], 0.0, BIG, ALU.is_equal, ALU.mult).then_inc(dist_mask, 1)
                dve.wait_ge(dist_mask, b + 1)
                for t in range(QT):
                    m = dve.tensor_tensor(neg_dist[:, t], kpos_in[:], neg_dist[:, t], ALU.subtract)
                m.then_inc(dist_plain, 1)
                dve.wait_ge(dist_plain, b + 1)
                dve.tensor_tensor(neg_dist, neg_dist, qpos_f[:, bass.ds(b, 1), :].rearrange("p b t -> p (b t)")
                                  .unsqueeze(2).to_broadcast((P, QT, NK)), ALU.subtract).then_inc(dist_ready, 1)

            def batch(b, ffn, last):
                f = sub(b, 1)

                def feed_forward(*steps):
                    if ffn:
                        for step, n in steps:
                            step(f, n)

                def after(*steps):
                    if not last:
                        for step, n in steps:
                            step(b + 1, n)

                for g in range(G):
                    bias(b, 0, g)
                reciprocals(b, 0, 0)
                reciprocals(b, 0, 1)
                for g in range(G):
                    bias(b, 1, g)
                attn_low(b, 0)
                reciprocals(b, 1, 0)
                reciprocals(b, 1, 1)
                feed_forward((finish, 0))
                for g in range(G):
                    bias(b, 2, g)
                residual(b, 0)
                statistics2(b, 0)
                normalise2(b, 0)
                feed_forward((finish, 1))
                attn_low(b, 1)
                reciprocals(b, 2, 0)
                after((statistics1, 0))
                reciprocals(b, 2, 1)
                bias(b, 3, 0)
                bias(b, 3, 1)
                residual(b, 1)
                bias(b, 3, 2)
                statistics2(b, 1)
                bias(b, 3, 3)
                normalise2(b, 1)
                mix(b, 0)
                feed_forward((finish, 2))
                attn_low(b, 2)
                reciprocals(b, 3, 0)
                after((normalise1, 0))
                reciprocals(b, 3, 1)
                feed_forward((finish, 3))
                after((statistics1, 1))
                after((statistics1, 2), (normalise1, 1))
                residual(b, 2)
                attn_low(b, 3)
                after((turn1_low, 0), (normalise1, 2), (turn1_low, 1))
                statistics2(b, 2)
                after((statistics1, 3))
                residual(b, 3)
                normalise2(b, 2)
                after((turn1_low, 2), (normalise1, 3))
                statistics2(b, 3)
                mix(b, 1)
                after((turn1_low, 3))
                normalise2(b, 3)
                mix(b, 2)
                if not last:
                    distances(b + 1)
                mix(b, 3)

            for t in range(QT):
                statistics1(0, t)
            for t in range(QT):
                normalise1(0, t)
                turn1_low(0, t)
            distances(0)
            dve.wait_ge(gates_ready, 2)
            batch(0, False, False)
            with dve.Fori(1, NB - 1) as b:
                batch(b, True, False)
            batch(NB - 1, True, True)
            for t in range(QT):
                finish(NB - 1, t)

        @block.gpsimd
        def _(pool):
            as_f32 = lambda ap: ap.bitcast(F32)
            pool.memset(ident[:], 0.0).then_inc(ident_zero, 1)
            pool.memset(power[:], -0.5).then_inc(ident_zero, 1)
            pool.wait_ge(ident_zero, 2)
            pool.affine_select(out=ident[:], in_=ident[:], compare_op=ALU.not_equal, fill=1.0, base=0,
                               pattern=[[-1, P]], channel_multiplier=1).then_inc(consts_ready, 1)

            def rstd1_of(b, t):
                pool.wait_ge(stats1_ready, b * QT + t + 1)
                apart(pool)
                pool.tensor_scalar(rstd1[:, t:t + 1], mv1[:, t, 1:2], EPS, None, ALU.add).then_inc(var1_ready, 1)
                pool.wait_ge(var1_ready, b * QT + t + 1)
                pool.tensor_tensor(rstd1[:, t:t + 1], rstd1[:, t:t + 1], power[:], ALU.pow).then_inc(rstd1_ready, 1)

            def rstd2_of(b, t):
                pool.wait_ge(stats2_ready, b * QT + t + 1)
                apart(pool)
                pool.tensor_scalar(rstd2[:], mv2[:, 1:2], EPS, None, ALU.add).then_inc(var2_ready, 1)
                pool.wait_ge(var2_ready, b * QT + t + 1)
                pool.tensor_tensor(rstd2[:], rstd2[:], power[:], ALU.pow).then_inc(rstd2_ready, 1)

            def normalise_probs(b, t, half):
                heads = slice(half * H // 2, (half + 1) * H // 2)
                pool.wait_ge(recip_ready, (b * QT + t) * 2 + half + 1)
                part = probs[:, t % 2, heads, :]
                pool.tensor_tensor(part, part, recip[:, t % 2, heads].unsqueeze(2).to_broadcast((P, H // 2, NK)), ALU.mult)\
                    .then_inc(probs_ready, 1)

            def edge(b, t):
                pool.wait_ge(read["turn2"], b * QT + t + 1)
                if t > 0:
                    apart(pool)
                    pool.tensor_copy(xn2t[:, t % 2, :, 0:1], xn2t[:, (t - 1) % 2, :, P:P + 1]).then_inc(edge_ready, 1)
                elif not (isinstance(b, int) and b == 0):
                    apart(pool)
                    pool.memset(xn2t[:, 0, :, 0:1], 0.0).then_inc(edge_ready, 1)

            def difference(b, t):
                pool.wait_ge(edge_ready, b * QT + t + 1)
                if not (isinstance(b, int) and b == 0 and t == 0):
                    pool.wait_ge(mixg_low, b * QT + t)
                pool.tensor_tensor(diff[:], xn2t[:, t % 2, :, 1:], xn2t[:, t % 2, :, 0:P], ALU.subtract)\
                    .then_inc(diff_ready, 1)

            def mix_low(b, t):
                tokens = slice(t * P, (t + 1) * P)
                pool.wait_ge(mixk_high, b * QT + t + 1)
                pool.tensor_tensor(mixed_key[:, LO, :, tokens], mix_k[:], as_f32(mixed_key[:, HI, :, tokens]),
                                   ALU.subtract).then_inc(mixk_low, 1)
                pool.wait_ge(mixg_high, b * QT + t + 1)
                pool.tensor_tensor(mixed_gate[:, LO, :, tokens], diff[:], as_f32(mixed_gate[:, HI, :, tokens]),
                                   ALU.subtract).then_inc(mixg_low, 1)

            def squared_relu(b, m):
                pool.wait_ge(read["key"], b * CT + m + 1)
                if m > 0:
                    pool.wait_ge(act_low, b * CT + m)
                pool.tensor_tensor(square[:], relu[:], relu[:], ALU.mult).then_inc(square_ready, 1)
                pool.wait_ge(act_high, b * CT + m + 1)
                pool.tensor_tensor(xnt_or_act[:, LO, m, :], square[:], as_f32(xnt_or_act[:, HI, m, :]),
                                   ALU.subtract).then_inc(act_low, 1)

            def batch(b, ffn, last):
                f = sub(b, 1)

                def feed_forward(*steps):
                    if ffn:
                        for step, n in steps:
                            step(f, n)

                def after(*steps):
                    if not last:
                        for step, n in steps:
                            step(b + 1, n)

                feed_forward((squared_relu, 0), (squared_relu, 1))
                normalise_probs(b, 0, 0)
                feed_forward((squared_relu, 2))
                normalise_probs(b, 0, 1)
                feed_forward((squared_relu, 3))
                normalise_probs(b, 1, 0)
                normalise_probs(b, 1, 1)
                rstd2_of(b, 0)
                normalise_probs(b, 2, 0)
                after((rstd1_of, 0))
                normalise_probs(b, 2, 1)
                rstd2_of(b, 1)
                edge(b, 0)
                difference(b, 0)
                normalise_probs(b, 3, 0)
                normalise_probs(b, 3, 1)
                mix_low(b, 0)
                after((rstd1_of, 1), (rstd1_of, 2))
                edge(b, 1)
                difference(b, 1)
                rstd2_of(b, 2)
                after((rstd1_of, 3))
                rstd2_of(b, 3)
                edge(b, 2)
                mix_low(b, 1)
                difference(b, 2)
                mix_low(b, 2)
                edge(b, 3)
                difference(b, 3)
                mix_low(b, 3)

            pool.wait_ge(consts_ready, 2)
            for t in range(QT):
                rstd1_of(0, t)
            batch(0, False, False)
            with pool.Fori(1, NB - 1) as b:
                batch(b, True, False)
            batch(NB - 1, True, True)
            for m in range(CT):
                squared_relu(NB - 1, m)


def kernel(x, ctx_1024, itok_BxS_8_8191, itok_BxS2_1_8191, mask_BxSxS2_if1, g_xattn, g_ffn,
           L0_xattn_W_q, L0_xattn_W_k, L0_xattn_W_v, L0_xattn_W_o, L0_ffn_W_r, L0_ffn_W_k, L0_ffn_W_v,
           L0_ffn_mu_r, L0_ffn_mu_k):
    import concourse.bacc as bacc
    from concourse.bass_utils import run_bass_kernel_spmd

    per_partition = lambda a: np.asarray(a).reshape(-1, P).T
    arrays = {
        "x": x, "ctx_t": np.asarray(ctx_1024).reshape(-1, np.asarray(ctx_1024).shape[-1]).T,
        "qpos": per_partition(itok_BxS_8_8191), "kpos": itok_BxS2_1_8191, "mask": mask_BxSxS2_if1,
        "g_xattn": g_xattn, "g_ffn": g_ffn,
        "wq": np.asarray(L0_xattn_W_q).T, "wk": np.asarray(L0_xattn_W_k).T, "wv": np.asarray(L0_xattn_W_v).T,
        "wo": np.asarray(L0_xattn_W_o).T, "ffn_wr": np.asarray(L0_ffn_W_r).T, "ffn_wk": np.asarray(L0_ffn_W_k).T,
        "ffn_wv": np.asarray(L0_ffn_W_v).T, "mu_r": per_partition(L0_ffn_mu_r), "mu_k": per_partition(L0_ffn_mu_k),
    }
    nc = bacc.Bacc("TRN2", target_bir_lowering=False, num_devices=1)
    feeds, args = {}, []
    for name, a in arrays.items():
        a = np.ascontiguousarray(a)
        feeds[f"in_{name}_dram"] = a
        args.append(nc.dram_tensor(f"in_{name}_dram", a.shape, mybir.dt.from_np(a.dtype), kind="ExternalInput").ap())
    out = nc.dram_tensor("out_dram", x.shape, F32, kind="ExternalOutput").ap()
    flamingo_block(nc, *args, out)
    result = run_bass_kernel_spmd(nc, [feeds], core_ids=[0])
    return result.results[0]["out_dram"]
```

```python
from contextlib import ExitStack

import numpy as np

import concourse.bass as bass
from concourse import mybir

F32 = mybir.dt.float32
F32R = mybir.dt.float32r
I32 = mybir.dt.int32
ALU = mybir.AluOpType
ACT = mybir.ActivationFunctionType
AX = mybir.AxisListType

P = 128
HI, LO = 0, 1

SPLIT_PASSES = ((HI, HI), (HI, LO), (LO, HI))

ATTENTION_AND_FFN = (
    ("gate", 0, -1), ("gate", 1, -1), ("key", 0, -1), ("key", 1, -1), ("key", 2, -1), ("key", 3, -1),
    ("proj", 0, 0), ("value", 0, -1), ("value", 1, -1), ("gate", 2, -1), ("turn2", 0, 0), ("proj", 1, 0),
    ("value", 2, -1), ("gate", 3, -1), ("proj", 2, 0), ("turn1", 1, 1),
    ("value", 3, -1), ("proj", 3, 0), ("query", 0, 1), ("query", 1, 1), ("query", 2, 1), ("query", 3, 1),
)
LATE_USES = (("gate", 1), ("key", 0), ("key", 1), ("key", 2), ("key", 3), ("value", 0), ("value", 1), ("value", 2))
LATE_PER_CHUNK = 4
SPARE_BANKS = {("turn1", 0): "score_bank0", ("turn2", 1): "score_bank1", ("turn1", 2): "probs_bank",
               ("turn2", 2): "attn_bank", ("turn1", 3): "attn_bank", ("turn2", 3): "probs_bank"}


def flamingo_block(nc, x, ctx_t, qpos, kpos, mask, g_xattn, g_ffn, wq, wk, wv, wo,
                   ffn_wr, ffn_wk, ffn_wv, mu_r, mu_k, out):
    NB, S, D = x.shape
    NK = kpos.shape[1]
    H = 16
    HD = D // H
    QT = S // P
    CT = D // P
    G = CT
    J = P // HD
    CB = 2
    CK = CB * NK
    EPS = 1e-5
    BIG = 1e30
    SCALE = 1.0 / float(np.sqrt(HD))
    RATIO = 2.0 ** (-8.0 / H)
    SLOPES = [float(np.float32(RATIO ** i)) for i in range(1, H + 1)]
    assert S == 512 and D == 512 and NB % (2 * CB) == 0 and NB >= 8 * CB

    key_scratch = nc.dram_tensor("key_scratch", (NB, P, CT, NK), F32, kind="Internal").ap()
    value_scratch = nc.dram_tensor("value_scratch", (NB, NK, D), F32, kind="Internal").ap()

    with ExitStack() as stack:
        def sb(name, shape, dt=F32):
            return stack.enter_context(nc.sbuf_tensor(name, shape, dt))

        def sem(name):
            return stack.enter_context(nc.semaphore(name))

        w_query, w_proj, w_gate, w_key, w_value = (
            sb(n, [P, 2, CT, D], F32R) for n in ("w_query", "w_proj", "w_gate", "w_key", "w_value"))
        xs = sb("xs", [P, 2, QT, D])
        norm1 = sb("norm1", [P, 2, D])
        norm2 = sb("norm2", [P, 2, D])
        xnt_or_act = sb("xnt_or_act", [P, 2, CT, S], F32R)
        mixed_key = sb("mixed_key", [P, 2, CT, S], F32R)
        mixed_gate = sb("mixed_gate", [P, 2, CT, S], F32R)
        xn2t = sb("xn2t", [P, 2, CT, 1 + P])
        diff = sb("diff", [P, CT, P])
        mix_k = sb("mix_k", [P, CT, P])
        query_t = sb("query_t", [P, CT, S])
        probs = sb("probs", [P, 2, H, NK])
        probs_t = sb("probs_t", [NK, 2, J, P])
        attn_t = sb("attn_t", [P, 2, G, P], F32R)
        keys_t = sb("keys_t", [P, CT, NK])
        values = sb("values", [NK, D])
        gated = sb("gated", [P, 2, D])
        relu = sb("relu", [P, S])
        square = sb("square", [P, S])
        mask_in = sb("mask_in", [P, QT, NK], I32)
        kpos_in = sb("kpos_in", [P, NK], I32)
        neg_dist = mask_in[:].bitcast(F32)
        qpos_in = sb("qpos_in", [P, NB, QT], I32)
        qpos_f = sb("qpos_f", [P, NB, QT])
        ident = sb("ident", [P, P])
        mu = sb("mu", [P, 2, CT])
        gates_in = sb("gates_in", [P, 2])
        gates = sb("gates", [P, 2])
        half_gate = sb("half_gate", [P, 1])
        stats1 = sb("stats1", [P, QT, 6])
        stats2 = sb("stats2", [P, 6])
        mv1 = sb("mv1", [P, QT, 2])
        rstd1 = sb("rstd1", [P, QT])
        mv2 = sb("mv2", [P, 2])
        rstd2 = sb("rstd2", [P, 1])
        power = sb("power", [P, 1])
        neg_max = sb("neg_max", [P, 2, H])
        sums = sb("sums", [P, 2, H])
        sums1 = sb("sums1", [P, 2, H])
        recip = sb("recip", [P, 2, H])

        diffs = [diff, relu[:].rearrange("p (c q) -> p c q", c=CT)]
        mix_ks = [mix_k, square[:].rearrange("p (c q) -> p c q", c=CT)]

        tail_relus = [relu, square]
        tail_squares = [norm1[:, i] for i in range(2)]

        wk_split = mixed_key
        wv_split = mixed_gate
        ctx_raw = probs[:].rearrange("p a h k -> p (a h k)").rearrange("p (a c k) -> p a c k", a=4, k=CK)
        ctx_split = [xnt_or_act[:].rearrange("p s c t -> p (s c t)")[:, i * 2 * CT * CK:(i + 1) * 2 * CT * CK]
                     .rearrange("p (s c k) -> p s c k", s=2, c=CT) for i in range(2)]
        key_out = query_t[:].rearrange("p c t -> p (c t)").rearrange("p (a c k) -> p a c k", a=2, c=CT)[:, :, :, 0:CK]
        value_out = gated
        late_raw = [xs[:, 1].rearrange("p t d -> p (t d)")[:, i * 2 * D:i * 2 * D + CT * CK]
                    .rearrange("p (c k) -> p c k", c=CT) for i in range(2)]
        late_key_out = [relu, square]

        score_banks = [stack.enter_context(nc.psum_tensor(f"score_bank{j}", [P, 512], F32)) for j in range(J)]
        rotating = [stack.enter_context(nc.psum_tensor(f"rotating{i}", [P, 512], F32)) for i in range(2)]
        probs_bank = stack.enter_context(nc.psum_tensor("probs_bank", [P, 512], F32))
        attn_bank = stack.enter_context(nc.psum_tensor("attn_bank", [P, 512], F32))
        bank_of = {(what, tile): rotating[i % 2] for i, (what, tile, _) in enumerate(ATTENTION_AND_FFN)}
        spare = {"score_bank0": score_banks[0], "score_bank1": score_banks[1], "probs_bank": probs_bank,
                 "attn_bank": attn_bank}
        bank_of.update({use: spare[name] for use, name in SPARE_BANKS.items()})
        tail_bank = {("gate", t): rotating[t % 2] for t in range(QT)}
        tail_bank.update({(what, n): score_banks[n] for what in ("key", "value") for n in range(4)})

        small_loaded = sem("small_loaded")
        first_half = sem("first_half")
        first_half_high = sem("first_half_high")
        raw_weight = [sem(f"raw_weight{i}") for i in range(2)]
        ctx_loaded = [sem(f"ctx_loaded{i}") for i in range(2)]
        x_loaded = [sem(f"x_loaded{t}") for t in range(QT)]
        mask_loaded = sem("mask_loaded")
        keys_loaded = sem("keys_loaded")
        values_loaded = sem("values_loaded")
        keys_stored = [sem(f"keys_stored{i}") for i in range(2)]
        gated_stored = [sem(f"gated_stored{i}") for i in range(2)]
        ident_zero = sem("ident_zero")
        ident_ready = sem("ident_ready")
        qpos_ready = sem("qpos_ready")
        gates_ready = sem("gates_ready")
        weight_high = sem("weight_high")
        weight_low = sem("weight_low")
        ctx_high = sem("ctx_high")
        ctx_low = sem("ctx_low")
        kproj_done = sem("kproj_done")
        kproj_read = sem("kproj_read")
        vproj_done = sem("vproj_done")
        vproj_read = sem("vproj_read")
        late_done = sem("late_done")
        late_read = sem("late_read")
        done = {k: sem(f"{k}_done") for k in ("key", "gate", "value", "proj", "query", "turn1", "turn2")}
        read = {k: sem(f"{k}_read") for k in ("key", "gate", "value", "proj", "query", "turn1", "turn2")}
        turn1_high = sem("turn1_high")
        scores_done = sem("scores_done")
        scores_biased = sem("scores_biased")
        max_ready = sem("max_ready")
        exp_done = sem("exp_done")
        sum_ready = sem("sum_ready")
        recip_ready = sem("recip_ready")
        probs_ready = sem("probs_ready")
        probs_turned = sem("probs_turned")
        probs_t_ready = sem("probs_t_ready")
        attn_done = sem("attn_done")
        attn_high = sem("attn_high")
        attn_read = sem("attn_read")
        dist_mask = sem("dist_mask")
        dist_plain = sem("dist_plain")
        dist_ready = sem("dist_ready")
        stats1_part = sem("stats1_part")
        stats1_ready = sem("stats1_ready")
        var1_ready = sem("var1_ready")
        rstd1_ready = sem("rstd1_ready")
        norm1_ready = sem("norm1_ready")
        x2_ready = sem("x2_ready")
        stats2_part = sem("stats2_part")
        stats2_ready = sem("stats2_ready")
        var2_ready = sem("var2_ready")
        rstd2_ready = sem("rstd2_ready")
        norm2_ready = sem("norm2_ready")
        edge_ready = sem("edge_ready")
        diff_ready = sem("diff_ready")
        mixg_ready = sem("mixg_ready")
        mixk_ready = sem("mixk_ready")
        mixg_high = sem("mixg_high")
        mixk_high = sem("mixk_high")
        mixg_low = sem("mixg_low")
        mixk_low = sem("mixk_low")
        square_ready = sem("square_ready")
        act_high = sem("act_high")
        act_low = sem("act_low")
        tail_relu_ready = sem("tail_relu_ready")
        gated_part = sem("gated_part")
        out_ready = sem("out_ready")

        raw = [wk, wv, wq, ffn_wk, ffn_wr, ffn_wv, wo]
        split = [wk_split, wv_split, w_query, w_key, w_gate, w_value, w_proj]
        NCHUNK = NB // CB
        EARLY = NCHUNK - 2
        PAIRS = EARLY // 2

        def earlier(b, t, back):
            return not isinstance(b, int) or b * QT + t >= back

        def apart(engine):
            engine.nop(nofuse=True)

        block = stack.enter_context(nc.Block())

        @block.sync
        def _(sp):
            def load_weight(i):
                if i >= 2:
                    sp.wait_ge(weight_low, i - 1)
                sp.dma_start(xs[:, i % 2], raw[i].rearrange("(c p) n -> p c n", p=P)).then_inc(raw_weight[i % 2], 16)

            def load_ctx(chunk, i, wait=None):
                if wait is not None:
                    sp.wait_ge(ctx_low, wait)
                sp.dma_start(ctx_raw[:, i], ctx_t[:, bass.ds(chunk * CK, CK)].rearrange("(c p) k -> p c k", p=P))\
                    .then_inc(ctx_loaded[i], 16)

            def store_chunk(n, i):
                sp.wait_ge(kproj_read, n * 2 * CT + (i + 1) * CT)
                for b in range(CB):
                    sp.dma_start(key_scratch[bass.ds((n * 2 + i) * CB + b, 1)].rearrange("b p c k -> p (b c) k"),
                                 key_out[:, i, :, b * NK:(b + 1) * NK]).then_inc(keys_stored[i], 16)
                for b in range(CB):
                    sp.wait_ge(vproj_read, n * 2 * CB + i * CB + b + 1)
                    sp.dma_start(value_scratch[bass.ds((n * 2 + i) * CB + b, 1)].rearrange("b k d -> (b k) d"),
                                 value_out[0:NK, b, :]).then_inc(gated_stored[b], 16)

            def load_x(b, t):
                sp.dma_start(xs[:, bass.ds(b % 2, 1), t].rearrange("p a d -> p (a d)"),
                             x[bass.ds(b, 1), t * P:(t + 1) * P, :].rearrange("b p d -> (b p) d"))\
                    .then_inc(x_loaded[t], 16)

            def load_mask(b):
                sp.dma_start(mask_in[:], mask[bass.ds(b, 1)].rearrange("b (t p) k -> p (b t) k", p=P))\
                    .then_inc(mask_loaded, 16)
                sp.dma_start(kpos_in[:], kpos[bass.ds(b, 1)].to_broadcast((P, NK))).then_inc(mask_loaded, 16)

            def load_keys(b):
                sp.dma_start(keys_t[:], key_scratch[bass.ds(b, 1)].rearrange("b p c k -> p (b c) k"))\
                    .then_inc(keys_loaded, 16)

            def load_values(b):
                sp.dma_start(values[:], value_scratch[bass.ds(b, 1)].rearrange("b k d -> (b k) d"))\
                    .then_inc(values_loaded, 16)

            def store_out(b, t):
                sp.dma_start(out[bass.ds(b, 1), t * P:(t + 1) * P, :].rearrange("b p d -> (b p) d"),
                             gated[:, t % 2]).then_inc(gated_stored[t % 2], 16)

            load_ctx(0, 0)
            for half in range(2):
                tiles = slice(half * CT // 2, (half + 1) * CT // 2)
                sp.dma_start(xs[:, 0, tiles], raw[0].rearrange("(c p) n -> p c n", p=P)[:, tiles])\
                    .then_inc(raw_weight[0] if half else first_half, 16)
            load_weight(1)
            for dst, src in ((qpos_in[:].rearrange("p b t -> p (b t)"), qpos), (mu[:, 0, :], mu_r), (mu[:, 1, :], mu_k),
                             (gates_in[:, 0:1], g_xattn.rearrange("(a n) -> a n", a=1).to_broadcast((P, 1))),
                             (gates_in[:, 1:2], g_ffn.rearrange("(a n) -> a n", a=1).to_broadcast((P, 1)))):
                sp.dma_start(dst, src).then_inc(small_loaded, 16)
            load_ctx(1, 1)
            load_weight(2)
            load_weight(3)
            load_ctx(2, 0, wait=1)
            load_weight(4)
            load_weight(5)
            load_ctx(3, 1, wait=2)
            load_weight(6)
            store_chunk(0, 0)
            store_chunk(0, 1)
            sp.wait_ge(weight_low, len(raw))
            for t in range(QT):
                load_x(0, t)
            load_mask(0)
            sp.wait_ge(keys_stored[0], 16 * CB)
            sp.wait_ge(gated_stored[0], 16)
            load_keys(0)
            load_values(0)
            with sp.Fori(1, PAIRS - 1) as n:
                for i in range(2):
                    load_ctx(n * 2 + 2 + i, i, wait=n * 2 + i + 1)
                    store_chunk(n, i)
            for i in range(2):
                sp.dma_start(late_raw[i], ctx_t[:, (EARLY + i) * CK:(EARLY + i + 1) * CK]
                             .rearrange("(c p) k -> p c k", p=P)).then_inc(ctx_loaded[i], 16)
                store_chunk(PAIRS - 1, i)

            def store_late_chunk(i):
                sp.wait_ge(late_read, i * LATE_PER_CHUNK + 2)
                first = (EARLY + i) * CB
                for pair in range(2):
                    made = late_key_out[pair][:, 0:2 * CK].rearrange("p (c b k) -> p c b k", c=2, b=CB)
                    for b in range(CB):
                        sp.dma_start(key_scratch[first + b, :, pair * 2:pair * 2 + 2, :], made[:, :, b])\
                            .then_inc(keys_stored[i], 16)
                for b in range(CB):
                    sp.wait_ge(late_read, i * LATE_PER_CHUNK + 3 + b)
                    sp.dma_start(value_scratch[first + b], value_out[0:NK, b, :]).then_inc(gated_stored[b], 16)

            def batch(b, ffn, last):
                if not ffn:
                    sp.wait_ge(ctx_low, NCHUNK)
                    for t in range(QT):
                        load_x(b + 1, t)
                    store_late_chunk(0)
                    store_late_chunk(1)
                for t in range(QT):
                    if ffn:
                        sp.wait_ge(out_ready, (b - 1) * QT + t + 1)
                        if not last:
                            load_x(b + 1, t)
                        store_out(b - 1, t)
                    if t == 1 and not last:
                        sp.wait_ge(scores_biased, (b + 1) * QT * G)
                        load_mask(b + 1)
                        load_keys(b + 1)
                if not last:
                    sp.wait_ge(attn_done, (b + 1) * QT)
                    load_values(b + 1)

            batch(0, False, False)
            for i in range(2):
                sp.wait_ge(keys_stored[i], 16 * CB * (PAIRS + 2))
                sp.wait_ge(gated_stored[i], 16 * NCHUNK)
            with sp.Fori(1, NB - 1) as b:
                batch(b, True, False)
            batch(NB - 1, True, True)
            for t in range(QT):
                sp.wait_ge(out_ready, (NB - 1) * QT + t + 1)
                store_out(NB - 1, t)
            for i in range(2):
                sp.wait_ge(gated_stored[i], 16 * (NCHUNK + NB * QT // 2))

        @block.tensor
        def _(pe):
            MATMULS = CT * len(SPLIT_PASSES)

            def product(bank, stationary, moving, steps=range(MATMULS)):
                for i in steps:
                    c, (a, b) = i // len(SPLIT_PASSES), SPLIT_PASSES[i % len(SPLIT_PASSES)]
                    mm = pe.matmul(bank, stationary(a, c), moving(b, c), start=(i == 0), stop=(i == MATMULS - 1))
                return mm


            def chunk(n, i, first):
                pe.wait_ge(ctx_low, n * 2 + i + 1)
                for m in range(CT):
                    if not first:
                        pe.wait_ge(kproj_read, n * 2 * CT + i * CT - CT + m + 1)
                    product(score_banks[m][:, 0:CK], lambda s, c: wk_split[:, s, c, m * P:(m + 1) * P],
                            lambda s, c: ctx_split[i][:, s, c, :]).then_inc(kproj_done, 1)
                if first:
                    pe.wait_ge(weight_low, 2)
                for b in range(CB):
                    if not first:
                        pe.wait_ge(vproj_read, n * 2 * CB + i * CB - CB + b + 1)
                    product(rotating[b][0:NK, :], lambda s, c: ctx_split[i][:, s, c, b * NK:(b + 1) * NK],
                            lambda s, c: wv_split[:, s, c, :]).then_inc(vproj_done, 1)

            pe.wait_ge(weight_low, 1)
            chunk(0, 0, True)
            chunk(0, 1, False)
            with pe.Fori(1, PAIRS) as n:
                chunk(n, 0, False)
                chunk(n, 1, False)

            def free_bank(b, use, order, before):
                bank = bank_of[use[:2]]
                uses = [(u, 0) for u in order[:order.index(use)] if bank_of[u[:2]] is bank]
                if not uses:
                    uses = [(u, -1) for u in before if bank_of[u[:2]] is bank]
                if uses:
                    (what, n, rel), back = uses[-1]
                    if isinstance(b, int) and b == 0 and rel < 0:
                        pe.wait_ge(late_read, LATE_USES.index((what, n)) + 1)
                    else:
                        pe.wait_ge(read[what], (b + rel + back) * 4 + n + 1)

            def scores(b, t, g):
                if t % 2 == 0 and g % 2 == 0:
                    pe.wait_ge(read["query"], b * 4 + t + g // 2 + 1)
                if t == 0 and g == 0:
                    pe.wait_ge(keys_loaded, b * 16 + 16)
                if g == 0 and earlier(b, t, 1):
                    pe.wait_ge(scores_biased, (b * QT + t) * G)
                if g == 0 and t == 0 and earlier(b, t, 1):
                    pe.wait_ge(read["turn2"], b * QT - 2)
                for j in range(J):
                    rows = slice(j * HD, (j + 1) * HD)
                    mm = pe.matmul(score_banks[j][:, g * NK:(g + 1) * NK], query_t[rows, g, t * P:(t + 1) * P],
                                   keys_t[rows, g, :], start=True, stop=True)
                if g == G - 1:
                    mm.then_inc(scores_done, 1)

            def free_spare(b, use, last):
                what, tile = use
                if SPARE_BANKS[use].startswith("score_bank"):
                    pe.wait_ge(scores_biased, (b + 1) * QT * G)
                elif use == ("turn1", 3):
                    pe.wait_ge(read["turn2"], b * QT + 3)
                elif use == ("turn2", 3):
                    if not last:
                        pe.wait_ge(read["turn1"], (b + 1) * QT + 3)
                elif what == "turn1":
                    pe.wait_ge(probs_t_ready, (b + 1) * QT * G)
                else:
                    pe.wait_ge(attn_read, (b + 1) * QT)

            def turn1(b, t, steps):
                pe.wait_ge(norm1_ready, b * QT + t + 1)
                for c in range(CT):
                    channels = slice(c * P, (c + 1) * P)
                    mm = pe.transpose(bank_of["turn1", t][:, channels], norm1[:, t % 2, channels], ident[:])
                return mm

            def turn2(b, t, steps):
                pe.wait_ge(norm2_ready, b * QT + t + 1)
                for c in range(CT):
                    channels = slice(c * P, (c + 1) * P)
                    mm = pe.transpose(bank_of["turn2", t][:, channels], norm2[:, t % 2, channels], ident[:])
                return mm

            def query(b, u, steps):
                half, pair = divmod(u, 2)
                pe.wait_ge(read["turn1"], b * QT + (half + 1) * QT // 2)
                for n in range(2 * steps[0], 2 * steps[-1] + 2):
                    i, step = divmod(n, MATMULS)
                    m = pair * 2 + i
                    mm = product(bank_of["query", u][:, i * S // 2:(i + 1) * S // 2],
                                 lambda s, c: w_query[:, s, c, m * P:(m + 1) * P],
                                 lambda s, c: xnt_or_act[:, s, c, half * S // 2:(half + 1) * S // 2], [step])
                return mm

            def key(b, m, steps, banks=bank_of):
                if m == 0 and steps[0] == 0:
                    pe.wait_ge(mixk_low, (b + 1) * QT)
                return product(banks["key", m][:], lambda s, c: w_key[:, s, c, m * P:(m + 1) * P],
                               lambda s, c: mixed_key[:, s, c, :], steps)

            def gate(b, t, steps, banks=bank_of):
                if steps[0] == 0:
                    pe.wait_ge(mixg_low, b * QT + t + 1)
                return product(banks["gate", t][:], lambda s, c: mixed_gate[:, s, c, t * P:(t + 1) * P],
                               lambda s, c: w_gate[:, s, c, :], steps)

            def value(b, t, steps, banks=bank_of):
                if t == 0 and steps[0] == 0:
                    pe.wait_ge(act_low, (b + 1) * CT)
                return product(banks["value", t][:], lambda s, c: xnt_or_act[:, s, c, t * P:(t + 1) * P],
                               lambda s, c: w_value[:, s, c, :], steps)

            def proj(b, t, steps):
                if steps[0] == 0:
                    pe.wait_ge(attn_read, b * QT + t + 1)
                return product(bank_of["proj", t][:], lambda s, c: attn_t[:, s, c, :],
                               lambda s, c: w_proj[:, s, c, :], steps)

            def late_product(use, steps):
                i, part = divmod(LATE_USES.index(use), LATE_PER_CHUNK)
                if steps[0] == 0:
                    pe.wait_ge(ctx_low, EARLY + i + 1)
                if part >= 2:
                    b = part - 2
                    return product(bank_of[use][0:NK, :], lambda s, c: ctx_split[i][:, s, c, b * NK:(b + 1) * NK],
                                   lambda s, c: wv_split[:, s, c, :], steps)
                for n in range(2 * steps[0], 2 * steps[-1] + 2):
                    half, step = divmod(n, MATMULS)
                    m = part * 2 + half
                    mm = product(bank_of[use][:, half * CK:(half + 1) * CK],
                                 lambda s, c: wk_split[:, s, c, m * P:(m + 1) * P],
                                 lambda s, c: ctx_split[i][:, s, c, :], [step])
                return mm

            made = {"key": key, "gate": gate, "value": value, "proj": proj, "turn1": turn1, "turn2": turn2,
                    "query": query}

            def turn_probs(b, t, g):
                pe.wait_ge(probs_ready, (b * QT + t) * 2 + g // 2 + 1)
                if g > 0 or earlier(b, t, 1):
                    pe.wait_ge(probs_t_ready, (b * QT + t) * G + g)
                    if t == 0 and g == 0:
                        pe.wait_ge(read["turn2"], b * QT)
                for j in range(J):
                    mm = pe.transpose(probs_bank[0:NK, j * P:(j + 1) * P], probs[:, t % 2, g * J + j, :], ident[:])
                mm.then_inc(probs_turned, 1)

            def attend(b, t, g):
                pe.wait_ge(probs_t_ready, (b * QT + t) * G + g + 1)
                if g == 0:
                    if t == 0:
                        pe.wait_ge(values_loaded, b * 16 + 16)
                    if earlier(b, t, 1):
                        pe.wait_ge(attn_read, b * QT + t)
                    if t == 0:
                        pe.wait_ge(read["turn1"], (b + 1) * QT)
                for j in range(J):
                    head = g * J + j
                    mm = pe.matmul(attn_bank[j * HD:(j + 1) * HD, g * P:(g + 1) * P],
                                   values[:, head * HD:(head + 1) * HD], probs_t[:, g % 2, j, :],
                                   start=True, stop=True, skip_group_check=True)
                if g == G - 1:
                    mm.then_inc(attn_done, 1)

            def batch(b, ffn, last, before):
                order = [u for u in ATTENTION_AND_FFN
                         if (ffn or u[2] >= 0 or u[:2] in LATE_USES) and (not last or u[2] <= 0)]

                def use(what, tile, steps=range(MATMULS)):
                    if (what, tile) in SPARE_BANKS:
                        if last and what == "turn1":
                            return
                        free_spare(b, (what, tile), last)
                        made[what](b + (what == "turn1"), tile, steps).then_inc(done[what], 1)
                        return
                    found = [u for u in order if u[:2] == (what, tile)]
                    if not found or not steps:
                        return
                    if steps[0] == 0:
                        free_bank(b, found[0], order, before)
                    late = not ffn and found[0][2] < 0
                    mm = late_product((what, tile), steps) if late else made[what](b + found[0][2], tile, steps)
                    if steps[-1] == MATMULS - 1:
                        mm.then_inc(late_done if late else done[what], 1)

                def with_scores(t, what, tile, portions):
                    at = 0
                    for g in range(G):
                        scores(b, t, g)
                        use(what, tile, range(at, at + portions[g]))
                        at += portions[g]

                def with_attention(t, what, tile, portions=(4, 3, 3, 2)):
                    at = 0
                    for g in range(G):
                        turn_probs(b, t, g)
                        use(what, tile, range(at, at + portions[g]))
                        at += portions[g]
                        if g > 0:
                            attend(b, t, g - 1)
                    attend(b, t, G - 1)

                with_scores(0, "gate", 0, (3, 3, 3, 3))
                use("gate", 1)
                use("key", 0)
                with_scores(1, "key", 1, (3, 3, 3, 3))
                with_attention(0, "key", 2)
                use("key", 3)
                with_scores(2, "proj", 0, (3, 3, 3, 3))
                use("value", 0)
                with_attention(1, "value", 1)
                with_scores(3, "gate", 2, (4, 4, 4, 0))
                use("turn2", 0)
                use("proj", 1)
                with_attention(2, "value", 2)
                use("gate", 3)
                use("turn1", 0)
                use("turn2", 1)
                with_attention(3, "proj", 2)
                use("turn1", 1)
                use("value", 3)
                use("proj", 3)
                use("turn1", 2)
                use("query", 0)
                if last:
                    pe.wait_ge(read["value"], b * QT)
                    gate(b, 0, range(MATMULS), tail_bank).then_inc(done["gate"], 1)
                use("turn2", 2)
                use("query", 1, range(7))
                use("turn1", 3)
                use("query", 1, range(7, MATMULS))
                use("turn2", 3)
                use("query", 2)
                use("query", 3)

            pe.wait_ge(kproj_read, EARLY * CT)
            pe.wait_ge(vproj_read, EARLY * CB)
            pe.wait_ge(ident_ready, 1)
            first = [u for u in ATTENTION_AND_FFN if u[0] in ("turn1", "query")]
            for t in range(QT):
                turn1(0, t, None).then_inc(done["turn1"], 1)
            for u in range(4):
                free_bank(-1, ("query", u, 1), first, [])
                query(0, u, range(MATMULS)).then_inc(done["query"], 1)
            batch(0, False, False, first)
            full = list(ATTENTION_AND_FFN)
            with pe.Fori(1, NB - 1) as b:
                batch(b, True, False, full)
            batch(NB - 1, True, True, full)
            f = NB - 1

            def tail(what, n):
                made[what](f, n, range(MATMULS), tail_bank).then_inc(done[what], 1)

            pe.wait_ge(read["proj"], NB * QT)
            tail("gate", 1)
            pe.wait_ge(scores_biased, NB * QT * G)
            for half in range(2):
                pe.wait_ge(mixk_low, f * QT + (half + 1) * QT // 2)
                for m in range(CT):
                    tokens = slice(half * S // 2, (half + 1) * S // 2)
                    mm = product(tail_bank["key", m][:, tokens], lambda s, c: w_key[:, s, c, m * P:(m + 1) * P],
                                 lambda s, c: mixed_key[:, s, c, tokens])
                    if half == 1:
                        mm.then_inc(done["key"], 1)
            for t in range(2, QT):
                pe.wait_ge(read["gate"], f * QT + t - 1)
                tail("gate", t)
            for t in range(QT):
                pe.wait_ge(act_low, f * CT + t + 1)
                tail("value", t)

        @block.scalar
        def _(act):
            def weight(i):
                act.wait_ge(raw_weight[i % 2], 16 * (i // 2 + 1))
                act.copy(split[i][:, HI], xs[:, i % 2]).then_inc(weight_high, 1)

            def chunk(n, i, first):
                act.wait_ge(ctx_loaded[i], 16 * n + 16)
                if not first:
                    act.wait_ge(vproj_done, n * 2 * CB + i * CB - CB)
                act.copy(ctx_split[i][:, HI], ctx_raw[:, i]).then_inc(ctx_high, 1)

            def keys_out(n, i, first):
                if not first:
                    act.wait_ge(keys_stored[i], 16 * CB * n)
                for m in range(CT):
                    act.wait_ge(kproj_done, n * 2 * CT + i * CT + m + 1)
                    act.copy(key_out[:, i, m, :], score_banks[m][:, 0:CK]).then_inc(kproj_read, 1)

            chunk(0, 0, True)
            act.wait_ge(first_half, 16)
            act.copy(split[0][:, HI, 0:CT // 2], xs[:, 0, 0:CT // 2]).then_inc(first_half_high, 1)
            act.wait_ge(raw_weight[0], 16)
            act.copy(split[0][:, HI, CT // 2:], xs[:, 0, CT // 2:]).then_inc(weight_high, 1)
            weight(1)
            chunk(0, 1, True)
            act.wait_ge(small_loaded, 16 * 5)
            act.activation(gates[:], gates_in[:], ACT.Tanh).then_inc(gates_ready, 1)
            act.wait_ge(gates_ready, 1)
            act.mul(half_gate[:], gates[:, 1:2], 0.5).then_inc(gates_ready, 1)
            weight(2)
            keys_out(0, 0, True)
            weight(3)
            chunk(1, 0, False)
            weight(4)
            keys_out(0, 1, True)
            weight(5)
            chunk(1, 1, False)
            weight(6)
            with act.Fori(1, PAIRS - 1) as n:
                for i in range(2):
                    keys_out(n, i, False)
                    chunk(n + 1, i, False)
            for i in range(2):
                keys_out(PAIRS - 1, i, False)

            def turn1_out(b, t):
                if isinstance(b, int) and b == 1:
                    act.wait_ge(late_done, len(LATE_USES))
                elif earlier(b, 0, 2 * QT):
                    act.wait_ge(done["value"], (b - 2) * QT + t + 1)
                act.wait_ge(done["turn1"], b * QT + t + 1)
                act.copy(xnt_or_act[:, HI, :, t * P:(t + 1) * P],
                         bank_of["turn1", t][:].rearrange("p (c q) -> p c q", c=CT)).then_inc(turn1_high, 1)

            def query_out(b, u):
                half, pair = divmod(u, 2)
                act.wait_ge(done["query"], b * 4 + u + 1)
                act.mul(query_t[:, pair * 2:pair * 2 + 2, half * S // 2:(half + 1) * S // 2],
                        bank_of["query", u][:].rearrange("p (m q) -> p m q", m=2), SCALE).then_inc(read["query"], 1)

            def exps(b, t, g, heads=range(J)):
                act.wait_ge(max_ready, (b * QT + t) * G + g + 1)
                for j in heads:
                    head = g * J + j
                    e = act.activation(probs[:, t % 2, head, :], probs[:, t % 2, head, :], ACT.Exp,
                                       bias=neg_max[:, t % 2, head:head + 1],
                                       accum_out=sums[:, t % 2, head:head + 1])
                if heads[-1] == J - 1:
                    e.then_inc(exp_done, 1)

            def probs_out(b, t, g):
                act.wait_ge(probs_turned, (b * QT + t) * G + g + 1)
                act.copy(probs_t[:, g % 2], probs_bank[0:NK, :].rearrange("k (j q) -> k j q", j=J))\
                    .then_inc(probs_t_ready, 1)

            def attn_out(b, t):
                act.wait_ge(attn_done, b * QT + t + 1)
                if earlier(b, t, 1):
                    act.wait_ge(done["proj"], b * QT + t)
                act.copy(attn_t[:, HI], attn_bank[:].rearrange("p (g q) -> p g q", g=G)).then_inc(attn_high, 1)

            def turn2_out(b, t):
                act.wait_ge(done["turn2"], b * QT + t + 1)
                if t > 0:
                    act.wait_ge(edge_ready, b * QT + t)
                if earlier(b, t, 2):
                    act.wait_ge(mixg_ready, b * QT + t - 1)
                act.copy(xn2t[:, t % 2, :, 1:], bank_of["turn2", t][:].rearrange("p (c q) -> p c q", c=CT))\
                    .then_inc(read["turn2"], 1)

            def mix_key_high(b, t):
                act.wait_ge(mixk_ready, b * QT + t + 1)
                act.copy(mixed_key[:, HI, :, t * P:(t + 1) * P], mix_ks[t % 2][:]).then_inc(mixk_high, 1)

            def mix_gate_high(b, t):
                act.wait_ge(mixg_ready, b * QT + t + 1)
                act.copy(mixed_gate[:, HI, :, t * P:(t + 1) * P], diffs[t % 2][:]).then_inc(mixg_high, 1)

            def relu_out(b, m):
                act.wait_ge(done["key"], b * CT + m + 1)
                if m == 0:
                    act.wait_ge(mixg_low, (b + 1) * QT)
                act.activation(relu[:], bank_of["key", m][:], ACT.Relu).then_inc(read["key"], 1)

            def act_split(b, m):
                act.wait_ge(square_ready, b * CT + m + 1)
                act.copy(xnt_or_act[:, HI, m, :], square[:]).then_inc(act_high, 1)

            def gate_out(b, t, banks=bank_of):
                act.wait_ge(done["gate"], b * QT + t + 1)
                act.wait_ge(gated_stored[t % 2], (NCHUNK + b * 2 + t // 2) * 16)
                act.activation(gated[:, t % 2], banks["gate", t][:], ACT.Tanh, scale=0.5).then_inc(read["gate"], 1)

            def late_out(n):
                i, part = divmod(n, LATE_PER_CHUNK)
                act.wait_ge(late_done, n + 1)
                if n > 0:
                    act.wait_ge(late_read, n)
                if part < 2:
                    if i == 1:
                        act.wait_ge(keys_stored[0], 16 * CB * (PAIRS + 2))
                    out_place, bank = late_key_out[part][:, 0:2 * CK], bank_of[LATE_USES[n]][:, 0:2 * CK]
                else:
                    act.wait_ge(gated_stored[part - 2], 16 * (EARLY + i))
                    out_place, bank = value_out[0:NK, part - 2, :], bank_of[LATE_USES[n]][0:NK, :]
                act.copy(out_place, bank).then_inc(late_read, 1)

            def batch(b, ffn, last):
                f = b - 1

                def feed_forward(*steps):
                    for step, n in steps:
                        if ffn:
                            step(f, n)
                        elif (step, n) in late:
                            late_out(late[step, n])

                def after(*steps):
                    if not last:
                        for step, n in steps:
                            step(b + 1, n)

                late = {(gate_out, 1): 0, (relu_out, 0): 1, (relu_out, 1): 2, (relu_out, 2): 3, (relu_out, 3): 4}
                front, back = range(J // 2), range(J // 2, J)
                feed_forward((gate_out, 0))
                exps(b, 0, 0)
                feed_forward((gate_out, 1))
                exps(b, 0, 1)
                exps(b, 0, 2)
                feed_forward((relu_out, 0))
                exps(b, 0, 3)
                feed_forward((act_split, 0), (relu_out, 1))
                probs_out(b, 0, 0)
                probs_out(b, 0, 1)
                feed_forward((act_split, 1))
                probs_out(b, 0, 2)
                probs_out(b, 0, 3)
                feed_forward((relu_out, 2))
                attn_out(b, 0)
                exps(b, 1, 0)
                feed_forward((act_split, 2), (relu_out, 3))
                exps(b, 1, 1, front)
                feed_forward((act_split, 3))
                exps(b, 1, 1, back)
                exps(b, 1, 2)
                exps(b, 1, 3)
                probs_out(b, 1, 0)
                probs_out(b, 1, 1)
                exps(b, 2, 0, front)
                probs_out(b, 1, 2)
                exps(b, 2, 0, back)
                probs_out(b, 1, 3)
                attn_out(b, 1)
                for g in range(1, G):
                    exps(b, 2, g)
                feed_forward((gate_out, 2))
                turn2_out(b, 0)
                exps(b, 3, 0)
                probs_out(b, 2, 0)
                exps(b, 3, 1, front)
                probs_out(b, 2, 1)
                exps(b, 3, 1, back)
                probs_out(b, 2, 2)
                exps(b, 3, 2, front)
                probs_out(b, 2, 3)
                exps(b, 3, 2, back)
                attn_out(b, 2)
                exps(b, 3, 3)
                feed_forward((gate_out, 3))
                probs_out(b, 3, 0)
                after((turn1_out, 0))
                probs_out(b, 3, 1)
                turn2_out(b, 1)
                probs_out(b, 3, 2)
                mix_key_high(b, 0)
                probs_out(b, 3, 3)
                mix_gate_high(b, 0)
                attn_out(b, 3)
                if last:
                    mix_key_high(b, 1)
                    mix_gate_high(b, 1)
                after((turn1_out, 1), (turn1_out, 2), (query_out, 0))
                turn2_out(b, 2)
                after((turn1_out, 3), (query_out, 1))
                if not last:
                    mix_key_high(b, 1)
                    mix_gate_high(b, 1)
                turn2_out(b, 3)
                after((query_out, 2))
                mix_key_high(b, 2)
                mix_gate_high(b, 2)
                after((query_out, 3))
                mix_key_high(b, 3)
                mix_gate_high(b, 3)

            act.wait_ge(vproj_done, EARLY * CB)
            for t in range(QT):
                turn1_out(0, t)
            for i in range(2):
                act.wait_ge(keys_stored[i], 16 * CB * PAIRS)
            for u in range(4):
                query_out(0, u)
            for i in range(2):
                act.wait_ge(ctx_loaded[i], 16 * (PAIRS + 1))
                act.copy(ctx_split[i][:, HI], late_raw[i]).then_inc(ctx_high, 1)
            batch(0, False, False)
            with act.Fori(1, NB - 1) as b:
                batch(b, True, False)
            batch(NB - 1, True, True)
            gate_out(NB - 1, 0, tail_bank)
            gate_out(NB - 1, 1, tail_bank)

            def tail_relu(m):
                act.wait_ge(done["key"], (NB - 1) * CT + m + 1)
                if m < 2:
                    act.wait_ge(mixg_low, NB * QT)
                else:
                    act.wait_ge(square_ready, (NB - 1) * CT + m - 1)
                act.activation(tail_relus[m % 2][:], tail_bank["key", m][:], ACT.Relu).then_inc(tail_relu_ready, 1)

            def tail_high(m):
                act.wait_ge(square_ready, (NB - 1) * CT + m + 1)
                act.copy(xnt_or_act[:, HI, m, :], tail_squares[m % 2]).then_inc(act_high, 1)

            tail_relu(0)
            for m in range(1, CT):
                tail_relu(m)
                tail_high(m - 1)
            tail_high(CT - 1)
            gate_out(NB - 1, 2, tail_bank)
            gate_out(NB - 1, 3, tail_bank)

        @block.vector
        def _(dve):
            as_f32 = lambda ap: ap.bitcast(F32)
            dve.memset(xn2t[:, 0, :, 0:1], 0.0).then_inc(edge_ready, 1)

            def weight(i):
                dve.wait_ge(weight_high, i + 1)
                dve.tensor_tensor(split[i][:, LO], xs[:, i % 2], as_f32(split[i][:, HI]), ALU.subtract)\
                    .then_inc(weight_low, 1)

            def chunk(n, i):
                dve.wait_ge(ctx_high, n * 2 + i + 1)
                dve.tensor_tensor(ctx_split[i][:, LO], ctx_raw[:, i], as_f32(ctx_split[i][:, HI]), ALU.subtract)\
                    .then_inc(ctx_low, 1)

            def values_out(n, i, first):
                for b in range(CB):
                    dve.wait_ge(vproj_done, n * 2 * CB + i * CB + b + 1)
                    if not first:
                        dve.wait_ge(gated_stored[b], (n * 2 + i) * 16)
                    dve.tensor_copy(value_out[0:NK, b, :], rotating[b][0:NK, :]).then_inc(vproj_read, 1)

            def x_tile(b, t):
                return xs[:, bass.ds(b % 2, 1), t].rearrange("p a d -> p (a d)")

            def statistics1(b, t):
                dve.wait_ge(x_loaded[t], b * 16 + 16)
                if earlier(b, 0, 1):
                    dve.wait_ge(stats1_ready, (b - 1) * QT + t + 1)
                    dve.wait_ge(norm1_ready, (b - 1) * QT + t + 1)
                apart(dve)
                dve.bn_stats(stats1[:, t, :], x_tile(b, t)).then_inc(stats1_part, 1)
                dve.wait_ge(stats1_part, b * QT + t + 1)
                apart(dve)
                dve.bn_aggr(mv1[:, t, :], stats1[:, t, :]).then_inc(stats1_ready, 1)

            def normalise1(b, t):
                dve.wait_ge(rstd1_ready, b * QT + t + 1)
                if earlier(b, t, 2):
                    dve.wait_ge(done["turn1"], b * QT + t - 1)
                dve.tensor_scalar(norm1[:, t % 2], x_tile(b, t), mv1[:, t, 0:1], rstd1[:, t:t + 1], ALU.subtract, ALU.mult)\
                    .then_inc(norm1_ready, 1)

            def turn1_low(b, t):
                dve.wait_ge(turn1_high, b * QT + t + 1)
                part = xnt_or_act[:, :, :, t * P:(t + 1) * P]
                dve.tensor_tensor(part[:, LO], bank_of["turn1", t][:].rearrange("p (c q) -> p c q", c=CT),
                                  as_f32(part[:, HI]), ALU.subtract).then_inc(read["turn1"], 1)

            def bias(b, t, g):
                if g == 0:
                    dve.wait_ge(scores_done, b * QT + t + 1)
                    if t == 0:
                        dve.wait_ge(dist_ready, b + 1)
                    if earlier(b, t, 2):
                        dve.wait_ge(probs_turned, (b * QT + t - 1) * G)
                        dve.wait_ge(exp_done, (b * QT + t - 1) * G)
                for j in range(J):
                    head = g * J + j
                    z = dve.scalar_tensor_tensor(out=probs[:, t % 2, head, :], in0=neg_dist[:, t, :], scalar=SLOPES[head],
                                                 in1=score_banks[j][:, g * NK:(g + 1) * NK], op0=ALU.mult, op1=ALU.add)
                z.then_inc(scores_biased, 1)
                dve.wait_ge(scores_biased, (b * QT + t) * G + g + 1)
                dve.tensor_reduce(neg_max[:, t % 2, g * J:(g + 1) * J], probs[:, t % 2, g * J:(g + 1) * J, :],
                                  AX.X, ALU.max, negate=True).then_inc(max_ready, 1)

            def reciprocals(b, t, half):
                heads = slice(half * H // 2, (half + 1) * H // 2)
                at = (b * QT + t) * 2 + half + 1
                dve.wait_ge(exp_done, (b * QT + t) * G + half * 2 + 2)
                if half == 0 and earlier(b, t, 2):
                    dve.wait_ge(probs_ready, (b * QT + t - 1) * 2)
                dve.tensor_scalar(sums1[:, t % 2, heads], sums[:, t % 2, heads], 1.0, None, ALU.add).then_inc(sum_ready, 1)
                dve.wait_ge(sum_ready, at)
                dve.reciprocal(recip[:, t % 2, heads], sums1[:, t % 2, heads]).then_inc(recip_ready, 1)

            def attn_low(b, t):
                dve.wait_ge(attn_high, b * QT + t + 1)
                dve.tensor_tensor(attn_t[:, LO], attn_bank[:].rearrange("p (g q) -> p g q", g=G), as_f32(attn_t[:, HI]),
                                  ALU.subtract).then_inc(attn_read, 1)

            def residual(b, t):
                dve.wait_ge(done["proj"], b * QT + t + 1)
                tile = x_tile(b, t)
                dve.scalar_tensor_tensor(out=tile, in0=bank_of["proj", t][:], scalar=gates[:, 0:1], in1=tile,
                                         op0=ALU.mult, op1=ALU.add).then_inc(read["proj"], 1)

            def statistics2(b, t):
                tile = x_tile(b, t)
                dve.wait_ge(read["proj"], b * QT + t + 1)
                if earlier(b, t, 1):
                    dve.wait_ge(stats2_ready, b * QT + t)
                apart(dve)
                dve.bn_stats(stats2[:], tile).then_inc(stats2_part, 1)
                dve.wait_ge(stats2_part, b * QT + t + 1)
                if earlier(b, t, 1):
                    dve.wait_ge(var2_ready, b * QT + t)
                    dve.wait_ge(norm2_ready, b * QT + t)
                apart(dve)
                dve.bn_aggr(mv2[:], stats2[:]).then_inc(stats2_ready, 1)

            def normalise2(b, t):
                dve.wait_ge(rstd2_ready, b * QT + t + 1)
                if earlier(b, t, 2):
                    dve.wait_ge(done["turn2"], b * QT + t - 1)
                dve.tensor_scalar(norm2[:, t % 2], x_tile(b, t), mv2[:, 0:1], rstd2[:], ALU.subtract, ALU.mult)\
                    .then_inc(norm2_ready, 1)

            def mix(b, t):
                dve.wait_ge(diff_ready, b * QT + t + 1)
                if earlier(b, t, 2):
                    dve.wait_ge(mixk_low, b * QT + t - 1)
                both, previous = diffs[t % 2], xn2t[:, t % 2, :, 0:P]
                for c in range(CT):
                    m = dve.scalar_tensor_tensor(out=mix_ks[t % 2][:, c, :], in0=both[:, c, :], scalar=mu[:, 1, c:c + 1],
                                                 in1=previous[:, c, :], op0=ALU.mult, op1=ALU.add)
                m.then_inc(mixk_ready, 1)
                dve.wait_ge(mixk_ready, b * QT + t + 1)
                for c in range(CT):
                    m = dve.scalar_tensor_tensor(out=both[:, c, :], in0=both[:, c, :], scalar=mu[:, 0, c:c + 1],
                                                 in1=previous[:, c, :], op0=ALU.mult, op1=ALU.add)
                m.then_inc(mixg_ready, 1)

            def finish(b, t, banks=bank_of):
                dve.wait_ge(read["gate"], b * QT + t + 1)
                dve.wait_ge(done["value"], b * QT + t + 1)
                dve.scalar_tensor_tensor(out=gated[:, t % 2], in0=gated[:, t % 2], scalar=1.0, in1=banks["value", t][:],
                                         op0=ALU.add, op1=ALU.mult).then_inc(read["value"], 1)
                dve.wait_ge(read["value"], b * QT + t + 1)
                dve.scalar_tensor_tensor(out=gated[:, t % 2], in0=gated[:, t % 2], scalar=half_gate[:], in1=x_tile(b, t),
                                         op0=ALU.mult, op1=ALU.add).then_inc(out_ready, 1)

            def late_out(n):
                i, part = divmod(n, LATE_PER_CHUNK)
                dve.wait_ge(late_done, n + 1)
                if n > 0:
                    dve.wait_ge(late_read, n)
                if part < 2:
                    if i == 1:
                        dve.wait_ge(keys_stored[0], 16 * CB * (PAIRS + 2))
                    out_place, bank = late_key_out[part][:, 0:2 * CK], bank_of[LATE_USES[n]][:, 0:2 * CK]
                else:
                    dve.wait_ge(gated_stored[part - 2], 16 * (EARLY + i))
                    out_place, bank = value_out[0:NK, part - 2, :], bank_of[LATE_USES[n]][0:NK, :]
                dve.tensor_copy(out_place, bank).then_inc(late_read, 1)

            def distances(b):
                dve.wait_ge(mask_loaded, b * 32 + 32)
                dve.tensor_scalar(neg_dist, mask_in[:], 0.0, BIG, ALU.is_equal, ALU.mult).then_inc(dist_mask, 1)
                dve.wait_ge(dist_mask, b + 1)
                for t in range(QT):
                    m = dve.tensor_tensor(neg_dist[:, t], kpos_in[:], neg_dist[:, t], ALU.subtract)
                m.then_inc(dist_plain, 1)
                dve.wait_ge(dist_plain, b + 1)
                dve.tensor_tensor(neg_dist, neg_dist, qpos_f[:, bass.ds(b, 1), :].rearrange("p b t -> p (b t)")
                                  .unsqueeze(2).to_broadcast((P, QT, NK)), ALU.subtract).then_inc(dist_ready, 1)

            def batch(b, ffn, last):
                f = b - 1
                late = {(finish, 0): 5, (finish, 1): 6, (finish, 2): 7}

                def feed_forward(*steps):
                    for step, n in steps:
                        if ffn:
                            step(f, n)
                        elif (step, n) in late:
                            late_out(late[step, n])

                def after(*steps):
                    if not last:
                        for step, n in steps:
                            step(b + 1, n)

                for g in range(G):
                    bias(b, 0, g)
                reciprocals(b, 0, 0)
                reciprocals(b, 0, 1)
                for g in range(G):
                    bias(b, 1, g)
                attn_low(b, 0)
                reciprocals(b, 1, 0)
                bias(b, 2, 0)
                residual(b, 0)
                reciprocals(b, 1, 1)
                bias(b, 2, 1)
                bias(b, 2, 2)
                bias(b, 2, 3)
                statistics2(b, 0)
                feed_forward((finish, 0))
                normalise2(b, 0)
                attn_low(b, 1)
                reciprocals(b, 2, 0)
                feed_forward((finish, 1))
                after((statistics1, 0))
                reciprocals(b, 2, 1)
                bias(b, 3, 0)
                bias(b, 3, 1)
                after((normalise1, 0))
                bias(b, 3, 2)
                residual(b, 1)
                statistics2(b, 1)
                reciprocals(b, 3, 0)
                bias(b, 3, 3)
                feed_forward((finish, 2))
                normalise2(b, 1)
                attn_low(b, 2)
                after((statistics1, 1))
                reciprocals(b, 3, 1)
                mix(b, 0)
                after((turn1_low, 0), (normalise1, 1), (statistics1, 2))
                residual(b, 2)
                attn_low(b, 3)
                if last:
                    statistics2(b, 2)
                    finish(f, 3)
                    normalise2(b, 2)
                    mix(b, 1)
                    residual(b, 3)
                    statistics2(b, 3)
                    normalise2(b, 3)
                    mix(b, 2)
                else:
                    after((turn1_low, 1), (normalise1, 2))
                    statistics2(b, 2)
                    feed_forward((finish, 3))
                    normalise2(b, 2)
                    residual(b, 3)
                    after((turn1_low, 2))
                    after((statistics1, 3))
                    statistics2(b, 3)
                    after((normalise1, 3))
                    normalise2(b, 3)
                    after((turn1_low, 3))
                    mix(b, 1)
                    mix(b, 2)
                    distances(b + 1)
                mix(b, 3)

            chunk(0, 0)
            dve.wait_ge(first_half_high, 1)
            dve.tensor_tensor(split[0][:, LO, 0:CT // 2], xs[:, 0, 0:CT // 2], as_f32(split[0][:, HI, 0:CT // 2]), ALU.subtract)
            dve.wait_ge(weight_high, 1)
            dve.tensor_tensor(split[0][:, LO, CT // 2:], xs[:, 0, CT // 2:], as_f32(split[0][:, HI, CT // 2:]), ALU.subtract)\
                .then_inc(weight_low, 1)
            weight(1)
            chunk(0, 1)
            dve.wait_ge(small_loaded, 16 * 5)
            dve.tensor_copy(qpos_f[:], qpos_in[:]).then_inc(qpos_ready, 1)
            weight(2)
            weight(3)
            values_out(0, 0, True)
            chunk(1, 0)
            weight(4)
            weight(5)
            values_out(0, 1, False)
            chunk(1, 1)
            weight(6)
            with dve.Fori(1, PAIRS - 1) as n:
                for i in range(2):
                    values_out(n, i, False)
                    chunk(n + 1, i)
            for t in range(QT):
                statistics1(0, t)
            normalise1(0, 0)
            normalise1(0, 1)
            dve.wait_ge(qpos_ready, 1)
            distances(0)
            dve.wait_ge(gates_ready, 2)
            for i in range(2):
                values_out(PAIRS - 1, i, False)
            normalise1(0, 2)
            normalise1(0, 3)
            turn1_low(0, 0)
            turn1_low(0, 1)
            turn1_low(0, 2)
            turn1_low(0, 3)
            for i in range(2):
                dve.wait_ge(ctx_high, EARLY + i + 1)
                dve.tensor_tensor(ctx_split[i][:, LO], late_raw[i], as_f32(ctx_split[i][:, HI]), ALU.subtract)\
                    .then_inc(ctx_low, 1)
            batch(0, False, False)
            with dve.Fori(1, NB - 1) as b:
                batch(b, True, False)
            batch(NB - 1, True, True)

            def tail_square(m):
                dve.wait_ge(tail_relu_ready, m + 1)
                if m >= 2:
                    dve.wait_ge(act_low, (NB - 1) * CT + m - 1)
                dve.tensor_tensor(tail_squares[m % 2], tail_relus[m % 2][:], tail_relus[m % 2][:], ALU.mult)\
                    .then_inc(square_ready, 1)

            def tail_low(m):
                dve.wait_ge(act_high, (NB - 1) * CT + m + 1)
                dve.tensor_tensor(xnt_or_act[:, LO, m, :], tail_squares[m % 2], as_f32(xnt_or_act[:, HI, m, :]),
                                  ALU.subtract).then_inc(act_low, 1)

            tail_square(0)
            for m in range(1, CT):
                tail_square(m)
                tail_low(m - 1)
            tail_low(CT - 1)
            for t in range(QT):
                finish(NB - 1, t, tail_bank)

        @block.gpsimd
        def _(pool):
            as_f32 = lambda ap: ap.bitcast(F32)
            pool.memset(ident[:], 0.0).then_inc(ident_zero, 1)
            pool.memset(power[:], -0.5).then_inc(ident_zero, 1)
            pool.wait_ge(ident_zero, 2)
            pool.affine_select(out=ident[:], in_=ident[:], compare_op=ALU.not_equal, fill=1.0, base=0,
                               pattern=[[-1, P]], channel_multiplier=1).then_inc(ident_ready, 1)

            def rstd1_of(b, t):
                pool.wait_ge(stats1_ready, b * QT + t + 1)
                apart(pool)
                pool.tensor_scalar(rstd1[:, t:t + 1], mv1[:, t, 1:2], EPS, None, ALU.add).then_inc(var1_ready, 1)
                pool.wait_ge(var1_ready, b * QT + t + 1)
                pool.tensor_tensor(rstd1[:, t:t + 1], rstd1[:, t:t + 1], power[:], ALU.pow).then_inc(rstd1_ready, 1)

            def rstd2_of(b, t):
                pool.wait_ge(stats2_ready, b * QT + t + 1)
                apart(pool)
                pool.tensor_scalar(rstd2[:], mv2[:, 1:2], EPS, None, ALU.add).then_inc(var2_ready, 1)
                pool.wait_ge(var2_ready, b * QT + t + 1)
                pool.tensor_tensor(rstd2[:], rstd2[:], power[:], ALU.pow).then_inc(rstd2_ready, 1)

            def normalise_probs(b, t, half):
                heads = slice(half * H // 2, (half + 1) * H // 2)
                pool.wait_ge(recip_ready, (b * QT + t) * 2 + half + 1)
                part = probs[:, t % 2, heads, :]
                pool.tensor_tensor(part, part, recip[:, t % 2, heads].unsqueeze(2).to_broadcast((P, H // 2, NK)), ALU.mult)\
                    .then_inc(probs_ready, 1)

            def edge(b, t):
                pool.wait_ge(read["turn2"], b * QT + t + 1)
                if t > 0:
                    apart(pool)
                    pool.tensor_copy(xn2t[:, t % 2, :, 0:1], xn2t[:, (t - 1) % 2, :, P:P + 1]).then_inc(edge_ready, 1)
                elif earlier(b, 0, 1):
                    apart(pool)
                    pool.memset(xn2t[:, 0, :, 0:1], 0.0).then_inc(edge_ready, 1)

            def difference(b, t):
                pool.wait_ge(edge_ready, b * QT + t + 1)
                if isinstance(b, int) and b == 0 and t == 1:
                    for i in range(2):
                        pool.wait_ge(keys_stored[i], 16 * CB * (PAIRS + 2))
                if earlier(b, t, 2):
                    pool.wait_ge(mixg_low, b * QT + t - 1)
                pool.tensor_tensor(diffs[t % 2][:], xn2t[:, t % 2, :, 1:], xn2t[:, t % 2, :, 0:P], ALU.subtract)\
                    .then_inc(diff_ready, 1)

            def mix_low(b, t):
                tokens = slice(t * P, (t + 1) * P)
                pool.wait_ge(mixk_high, b * QT + t + 1)
                pool.tensor_tensor(mixed_key[:, LO, :, tokens], mix_ks[t % 2][:], as_f32(mixed_key[:, HI, :, tokens]),
                                   ALU.subtract).then_inc(mixk_low, 1)
                pool.wait_ge(mixg_high, b * QT + t + 1)
                pool.tensor_tensor(mixed_gate[:, LO, :, tokens], diffs[t % 2][:], as_f32(mixed_gate[:, HI, :, tokens]),
                                   ALU.subtract).then_inc(mixg_low, 1)

            def squared_relu(b, m):
                pool.wait_ge(read["key"], b * CT + m + 1)
                if m > 0:
                    pool.wait_ge(act_low, b * CT + m)
                pool.tensor_tensor(square[:], relu[:], relu[:], ALU.mult).then_inc(square_ready, 1)
                pool.wait_ge(act_high, b * CT + m + 1)
                pool.tensor_tensor(xnt_or_act[:, LO, m, :], square[:], as_f32(xnt_or_act[:, HI, m, :]),
                                   ALU.subtract).then_inc(act_low, 1)

            def batch(b, ffn, last):
                f = b - 1

                def feed_forward(*steps):
                    if ffn:
                        for step, n in steps:
                            step(f, n)

                def after(*steps):
                    if not last:
                        for step, n in steps:
                            step(b + 1, n)

                normalise_probs(b, 0, 0)
                feed_forward((squared_relu, 0))
                normalise_probs(b, 0, 1)
                feed_forward((squared_relu, 1), (squared_relu, 2), (squared_relu, 3))
                normalise_probs(b, 1, 0)
                normalise_probs(b, 1, 1)
                rstd2_of(b, 0)
                normalise_probs(b, 2, 0)
                after((rstd1_of, 0))
                normalise_probs(b, 2, 1)
                edge(b, 0)
                difference(b, 0)
                rstd2_of(b, 1)
                normalise_probs(b, 3, 0)
                normalise_probs(b, 3, 1)
                after((rstd1_of, 1))
                edge(b, 1)
                difference(b, 1)
                after((rstd1_of, 2))
                mix_low(b, 0)
                rstd2_of(b, 2)
                if last:
                    mix_low(b, 1)
                after((rstd1_of, 3))
                rstd2_of(b, 3)
                edge(b, 2)
                difference(b, 2)
                if not last:
                    mix_low(b, 1)
                edge(b, 3)
                difference(b, 3)
                mix_low(b, 2)
                mix_low(b, 3)

            for t in range(QT):
                rstd1_of(0, t)
            batch(0, False, False)
            with pool.Fori(1, NB - 1) as b:
                batch(b, True, False)
            batch(NB - 1, True, True)


def kernel(x, ctx_1024, itok_BxS_8_8191, itok_BxS2_1_8191, mask_BxSxS2_if1, g_xattn, g_ffn,
           L0_xattn_W_q, L0_xattn_W_k, L0_xattn_W_v, L0_xattn_W_o, L0_ffn_W_r, L0_ffn_W_k, L0_ffn_W_v,
           L0_ffn_mu_r, L0_ffn_mu_k):
    import concourse.bacc as bacc
    from concourse.bass_utils import run_bass_kernel_spmd

    per_partition = lambda a: np.asarray(a).reshape(-1, P).T
    arrays = {
        "x": x, "ctx_t": np.asarray(ctx_1024).reshape(-1, np.asarray(ctx_1024).shape[-1]).T,
        "qpos": per_partition(itok_BxS_8_8191), "kpos": itok_BxS2_1_8191, "mask": mask_BxSxS2_if1,
        "g_xattn": g_xattn, "g_ffn": g_ffn,
        "wq": np.asarray(L0_xattn_W_q).T, "wk": np.asarray(L0_xattn_W_k).T, "wv": np.asarray(L0_xattn_W_v).T,
        "wo": np.asarray(L0_xattn_W_o).T, "ffn_wr": np.asarray(L0_ffn_W_r).T, "ffn_wk": np.asarray(L0_ffn_W_k).T,
        "ffn_wv": np.asarray(L0_ffn_W_v).T, "mu_r": per_partition(L0_ffn_mu_r), "mu_k": per_partition(L0_ffn_mu_k),
    }
    nc = bacc.Bacc("TRN2", target_bir_lowering=False, num_devices=1)
    feeds, args = {}, []
    for name, a in arrays.items():
        a = np.ascontiguousarray(a)
        feeds[f"in_{name}_dram"] = a
        args.append(nc.dram_tensor(f"in_{name}_dram", a.shape, mybir.dt.from_np(a.dtype), kind="ExternalInput").ap())
    out = nc.dram_tensor("out_dram", x.shape, F32, kind="ExternalOutput").ap()
    flamingo_block(nc, *args, out)
    result = run_bass_kernel_spmd(nc, [feeds], core_ids=[0])
    return result.results[0]["out_dram"]
```
